# Optimizing a Trainium2 kernel written in Bass

```python
import numpy as np
import jax
import jax.numpy as jnp

def _softmax(x, axis=-1):
    return jax.nn.softmax(x, axis=axis)

def _gelu(x):
    return jax.nn.gelu(x, approximate=True)

def _silu(x):
    return jax.nn.silu(x)

def _sigmoid(x):
    return jax.nn.sigmoid(x)

def _layernorm(x, axis=-1, eps=1e-05):
    m = jnp.mean(x, axis=axis, keepdims=True)
    v = jnp.var(x, axis=axis, keepdims=True)
    return (x - m) / jnp.sqrt(v + eps)

def _scatter_add(tgt, idx, src, axis=0):
    return tgt.at[idx].add(src)

def _segment_sum(src, seg, n):
    return jax.ops.segment_sum(src, seg, n)
kernel_name = 'mk_flamingo_gated_d1_seqx_r4_7792cc'

def setup_inputs(seed: int=0):
    np.random.seed(seed)
    _w = jnp.asarray

    def _rec_inputs():
        import jax
        import jax.numpy as jnp
        _rk = jax.random.key(seed)
        x = -0.0003929 + 0.9999 * jax.random.normal(jax.random.fold_in(_rk, 1), (16, 128, 1024), jnp.float32)
        _lenS = 128 - jax.random.randint(jax.random.fold_in(_rk, 7), (16,), 0, max(1, 128 // 4) + 1, jnp.int32)
        _lenS2 = 128 - jax.random.randint(jax.random.fold_in(_rk, 8), (16,), 0, max(1, 128 // 4) + 1, jnp.int32)
        _ctx_4096P = jax.random.normal(jax.random.fold_in(_rk, 11), (16, 16, 1024), jnp.float32)
        _ctx_4096c = jax.random.dirichlet(jax.random.fold_in(_rk, 511), 0.3 * jnp.ones((16,), jnp.float32), (16, 128))
        _ctx_4096t = jnp.einsum('bsk,bkd->bsd', _ctx_4096c, _ctx_4096P)
        _ctx_4096t = _ctx_4096t * jax.lax.rsqrt(jnp.mean(jnp.square(_ctx_4096t)) + 1e-12) * 0.953939
        ctx_4096 = 2.81802e-05 + 1.00001 * (_ctx_4096t + 0.3 * jax.random.normal(jax.random.fold_in(_rk, 611), (16, 128, 1024), jnp.float32))
        _g = jax.random.normal(jax.random.fold_in(_rk, 9001), (2, 1), jnp.float32)
        _g = jnp.sign(_g) * jnp.maximum(jnp.abs(_g), 1.0) + (_g == 0) * 1.0
        g_xattn = _g[0]
        g_ffn = _g[1]
        return (x, ctx_4096, g_xattn, g_ffn)
    x, ctx_4096, g_xattn, g_ffn = _rec_inputs()

    def _L0_xattn_setup():
        import jax, jax.numpy as jnp
        import numpy as np
        EMBED = 1024
        HEADS = 32
        GROUP = 4
        KV_HEADS = HEADS // GROUP
        HEAD_DIM = EMBED // HEADS
        B, S = (2, 512)
        key = jax.random.key(seed)
        ks = jax.random.split(key, 7)
        scale = 0.02
        return {'queries': jax.random.normal(ks[0], (B, S, EMBED), dtype=jnp.float32), 'keys': jax.random.normal(ks[1], (B, S, EMBED), dtype=jnp.float32), 'values': jax.random.normal(ks[2], (B, S, EMBED), dtype=jnp.float32), 'Wq': jax.random.normal(ks[3], (EMBED, EMBED), dtype=jnp.float32) * scale, 'Wk': jax.random.normal(ks[4], (EMBED, KV_HEADS * HEAD_DIM), dtype=jnp.float32) * scale, 'Wv': jax.random.normal(ks[5], (EMBED, KV_HEADS * HEAD_DIM), dtype=jnp.float32) * scale, 'Wo': jax.random.normal(ks[6], (EMBED, EMBED), dtype=jnp.float32) * scale}
    _L0_xattn_all = _L0_xattn_setup()
    _L0_xattn_in = {k: v for k, v in _L0_xattn_all.items() if k in ('Wq', 'Wk', 'Wv', 'Wo')}
    del _L0_xattn_all

    def _L0_ffn_setup():
        import jax, jax.numpy as jnp
        import numpy as np
        D = 1024
        F = 2752
        B, S = (4, 512)
        key = jax.random.key(seed)
        k_x, k_g, k_u, k_d = jax.random.split(key, 4)
        scale = 0.02
        return {'x': jax.random.normal(k_x, (B, S, D), dtype=jnp.float32), 'W_gate': jax.random.normal(k_g, (F, D), dtype=jnp.float32) * scale, 'W_up': jax.random.normal(k_u, (F, D), dtype=jnp.float32) * scale, 'W_down': jax.random.normal(k_d, (D, F), dtype=jnp.float32) * scale}
    _L0_ffn_all = _L0_ffn_setup()
    _L0_ffn_in = {k: v for k, v in _L0_ffn_all.items() if k in ('W_gate', 'W_up', 'W_down')}
    del _L0_ffn_all
    return {'x': x, 'ctx_4096': ctx_4096, 'g_xattn': g_xattn, 'g_ffn': g_ffn, 'L0_xattn_Wq': _L0_xattn_in['Wq'], 'L0_xattn_Wk': _L0_xattn_in['Wk'], 'L0_xattn_Wv': _L0_xattn_in['Wv'], 'L0_xattn_Wo': _L0_xattn_in['Wo'], 'L0_ffn_W_gate': _L0_ffn_in['W_gate'], 'L0_ffn_W_up': _L0_ffn_in['W_up'], 'L0_ffn_W_down': _L0_ffn_in['W_down']}

def reference(x, ctx_4096, g_xattn, g_ffn, L0_xattn_Wq, L0_xattn_Wk, L0_xattn_Wv, L0_xattn_Wo, L0_ffn_W_gate, L0_ffn_W_up, L0_ffn_W_down):
    import jax
    import jax.numpy as jnp

    def _L0_xattn_ref(queries, keys, values, Wq, Wk, Wv, Wo):
        import jax, jax.numpy as jnp
        import numpy as np
        EMBED = 1024
        HEADS = 32
        GROUP = 4
        KV_HEADS = HEADS // GROUP
        HEAD_DIM = EMBED // HEADS
        B, S = (2, 512)
        b, s, _ = queries.shape
        q = (queries @ Wq).reshape(b, s, KV_HEADS, GROUP, HEAD_DIM)
        k = (keys @ Wk).reshape(b, s, KV_HEADS, HEAD_DIM)
        v = (values @ Wv).reshape(b, s, KV_HEADS, HEAD_DIM)
        scale = 1.0 / jnp.sqrt(jnp.asarray(HEAD_DIM, dtype=q.dtype))
        scores = jnp.einsum('bqhgd,bkhd->bhgqk', q, k) * scale
        attn = jax.nn.softmax(scores, axis=-1)
        out = jnp.einsum('bhgqk,bkhd->bqhgd', attn, v)
        out = out.reshape(b, s, EMBED)
        return out @ Wo

    def _L0_ffn_ref(x, W_gate, W_up, W_down):
        import jax, jax.numpy as jnp
        import numpy as np
        D = 1024
        F = 2752
        B, S = (4, 512)
        out_shape = x.shape[:-1] + (W_down.shape[0],)
        xt = x.reshape(-1, x.shape[-1])
        up = xt @ W_up.T
        gate = jax.nn.silu(xt @ W_gate.T)
        y = gate * up @ W_down.T
        return y.reshape(out_shape)
    x = x + jnp.tanh(g_xattn[0]) * _L0_xattn_ref(_layernorm(x, axis=-1), ctx_4096, ctx_4096, L0_xattn_Wq, L0_xattn_Wk, L0_xattn_Wv, L0_xattn_Wo)
    x = x + jnp.tanh(g_ffn[0]) * _L0_ffn_ref(_layernorm(x, axis=-1), L0_ffn_W_gate, L0_ffn_W_up, L0_ffn_W_down)
    return x

_drawn_inputs = setup_inputs


def setup_inputs(seed=0):
    import zlib

    import numpy as np

    out = dict(_drawn_inputs(seed))
    spreads = {}
    factors = {}
    for name, (base, spread) in spreads.items():
        noise = np.random.default_rng([zlib.crc32(name.encode()), seed]).standard_normal(out[name].shape)
        drawn = base * np.exp(spread * noise) if base else spread * noise
        out[name] = jnp.asarray(drawn.astype(out[name].dtype))
    for name, factor in factors.items():
        out[name] = (out[name] * factor).astype(out[name].dtype)
    return out
```

```python
from contextlib import ExitStack

import concourse.bass as bass
from concourse import mybir

P = 128
BATCH, SEQ, D = 16, 128, 1024
HEADS, KV_HEADS, HD = 32, 8, 32
GQ = HEADS // KV_HEADS
F = 2752
EPS = 1e-5
SCALE = float(HD) ** -0.5

TOK = 512
NB = TOK // SEQ
NG = BATCH // NB
K8 = D // P
HALF = 512
NH = D // HALF

NQ = D // P
NKV = 2 * KV_HEADS * HD // P
FT = F // P
FR = F - FT * P
NC = NQ + NKV + 2 * FT + 1
WKV, WFF, WMIX = NQ, NQ + NKV, NC - 1
CS = 4
NO = D // P
NR = NO + FT + 1
RS = 4

UNITS = NB * NH * GQ
PAIRS = UNITS // 2
BLOCKS = 4
CHUNKS = (FT + 1) // 2
YN = NB * NH
LOOPS = 4
STEPS = UNITS + 3

F32 = mybir.dt.float32
F32R = mybir.dt.float32r
ACT = mybir.ActivationFunctionType
ALU = mybir.AluOpType
AX_X = mybir.AxisListType.X


def gated_cross_attention_ffn(nc, x, ctx_t, wc, wr, g_xattn, g_ffn, out):
    with ExitStack() as ctx:
        end = [(nc.sbuf_base + 31) // 32 * 32]

        def at(name, shape, dt, offset):
            return nc.alloc_sbuf_tensor_at(name, shape, dt, offset=offset)

        def sb(name, shape, dt=F32):
            size = 4
            for n in shape[1:]:
                size *= n
            offset = end[0]
            end[0] += (size + 31) // 32 * 32
            return at(name, shape, dt, offset), offset

        xt_h, _ = sb("xt_h", [P, K8, TOK], F32R)
        xt_l, _ = sb("xt_l", [P, K8, TOK], F32R)
        wc_h, _ = sb("wc_h", [P, CS, K8, P], F32R)
        wc_l, _ = sb("wc_l", [P, CS, K8, P], F32R)
        wc_raw, _ = sb("wc_raw", [P, 2, K8 * P])
        wr_h, _ = sb("wr_h", [P, RS, D], F32R)
        wr_l, _ = sb("wr_l", [P, RS, D], F32R)
        wr_raw, _ = sb("wr_raw", [P, D])
        kc_h, _ = sb("kc_h", [P, 2, TOK], F32R)
        kc_l, _ = sb("kc_l", [P, 2, TOK], F32R)
        vc_h, _ = sb("vc_h", [P, NB, 2 * P], F32R)
        vc_l, _ = sb("vc_l", [P, NB, 2 * P], F32R)
        qo_h, o_qh = sb("qo_h", [P, 2 * GQ, TOK], F32R)
        qo_l, o_ql = sb("qo_l", [P, 2 * GQ, TOK], F32R)
        h_h = at("h_h", [P, 4, TOK], F32R, o_qh)
        h_l = at("h_l", [P, 4, TOK], F32R, o_ql)
        x1, o_x1 = sb("x1", [P, NB, D])
        pt_h = at("pt_h", [P, 2, 4, 2 * P], F32R, o_x1)
        pt_l = at("pt_l", [P, 2, 4, 2 * P], F32R, o_x1 + 8192)
        xn, o_kb = sb("xn", [P, NB, D])
        kb_h = at("kb_h", [P, NB, HALF], F32R, o_kb)
        kb_l = at("kb_l", [P, NB, HALF], F32R, o_kb + 8192)
        ct_h = at("ct_h", [P, 2, K8, P], F32R, o_kb)
        ct_l = at("ct_l", [P, 2, K8, P], F32R, o_kb + 8192)
        ct_raw, o_vp = sb("ct_raw", [P, 2, K8 * P])
        vp_h = at("vp_h", [P, 2, 4, P], F32R, o_vp)
        vp_l = at("vp_l", [P, 2, 4, P], F32R, o_vp + 4096)
        pb, o_pb = sb("pb", [P, 4, HALF])
        xn2 = at("xn2", [P, 2, D], F32, o_pb)
        sg = at("sg", [P, 2, HALF], F32, o_pb)
        hf = at("hf", [P, 2, HALF], F32, o_pb + 4096)
        kn, _ = sb("kn", [P, 2, 2 * P])
        ident, _ = sb("ident", [P, P])
        nmx, _ = sb("nmx", [P, 4, 4])
        psum_, _ = sb("psum_", [P, 4, 4])
        rinv, _ = sb("rinv", [P, 4, 4])
        st, _ = sb("st", [P, 2, 12])
        mv, _ = sb("mv", [P, NB, 2])
        ve, _ = sb("ve", [P, NB])
        rstd, _ = sb("rstd", [P, NB])
        mhalf, _ = sb("mhalf", [P, 1])
        gates, _ = sb("gates", [P, 2])
        tg, _ = sb("tg", [P, 2])

        ps = ctx.enter_context(nc.psum_tensor("ps", [P, 8, HALF], F32))

        def sem(name):
            return ctx.enter_context(nc.semaphore(name))

        ident_zero = sem("ident_zero")
        consts = sem("consts")
        gates_in = sem("gates_in")
        wc_in = [sem("wc_in0"), sem("wc_in1")]
        wr_in = sem("wr_in")
        ct_in = [sem("ct_in0"), sem("ct_in1")]
        x1_in = sem("x1_in")
        xn_in = sem("xn_in")
        stored = sem("stored")
        wc_hi, wc_lo = sem("wc_hi"), sem("wc_lo")
        wr_hi, wr_lo = sem("wr_hi"), sem("wr_lo")
        ct_hi, ct_lo = sem("ct_hi"), sem("ct_lo")
        q_hi, q_lo = sem("q_hi"), sem("q_lo")
        pt_hi, pt_lo = sem("pt_hi"), sem("pt_lo")
        o_hi, o_lo = sem("o_hi"), sem("o_lo")
        v_hi, v_lo = sem("v_hi"), sem("v_lo")
        k_hi, k_lo = sem("k_hi"), sem("k_lo")
        xt1_hi, xt1_lo = sem("xt1_hi"), sem("xt1_lo")
        xt2_hi, xt2_lo = sem("xt2_hi"), sem("xt2_lo")
        h_hi, h_lo = sem("h_hi"), sem("h_lo")
        wc_used = sem("wc_used")
        o_first = sem("o_first")
        o_done = sem("o_done")
        s_done = sem("s_done")
        pt_done = sem("pt_done")
        pv_done = sem("pv_done")
        kv_done = sem("kv_done")
        kt_done = sem("kt_done")
        xt1_done, xt2_done = sem("xt1_done"), sem("xt2_done")
        y_done = sem("y_done")
        passed = sem("passed")
        tg_ready = sem("tg_ready")
        kb_zero = sem("kb_zero")
        kb_built = sem("kb_built")
        vp_built = sem("vp_built")
        maxed = sem("maxed")
        exped = sem("exped")
        inverted = sem("inverted")
        normed = sem("normed")
        k_nat = sem("k_nat")
        x1_add = sem("x1_add")
        st1, st2 = sem("st1"), sem("st2")
        mv1, mv2 = sem("mv1"), sem("mv2")
        ve_ready = sem("ve_ready")
        rs1, rs2 = sem("rs1"), sem("rs2")
        xn1_ready, xn2_ready = sem("xn1_ready"), sem("xn2_ready")
        gate_free = sem("gate_free")
        up_free = sem("up_free")
        y_free = sem("y_free")

        def wcn(g, i, last):
            return g * NC + (NKV + i - (NKV if last and i >= WFF else 0))

        def used(g, i):
            return g * (NC - NKV) + (i + 1 - (NKV if i >= WFF else 0))

        def wc_arrived(g, i, last):
            per = (NC + 1) // 2 if i % 2 == 0 else NC // 2
            before = 2 + i // 2 - (NKV // 2 if last and i >= WFF else 0)
            return g * (16 * per) + 16 * (before + 1)

        def ct_arrived(G, b):
            return G * 32 + 16 * (b // 2 + 1)

        block = ctx.enter_context(nc.Block())

        @block.sync
        def _(sp):
            def load_wc(g, i, last, src=None):
                if not (isinstance(g, int) and g == -1):
                    sp.wait_ge(wc_lo, wcn(g, i, last) - (0 if i == 0 else 1))
                sp.dma_start(wc_raw[:, i % 2, :], wc[i] if src is None else src).then_inc(wc_in[i % 2], 16)

            def load_wr(g, i, src=None):
                if i > 0:
                    sp.wait_ge(wr_lo, g * NR + i)
                sp.dma_start(wr_raw[:, :], wr[i] if src is None else src).then_inc(wr_in, 16)

            def load_ct(G, b, src):
                if b >= 2:
                    sp.wait_ge(ct_lo, G * NB + (b - 1))
                sp.dma_start(ct_raw[:, b % 2, :], src).then_inc(ct_in[b % 2], 16)

            def body(g, last):
                for i in (4, 5):
                    load_wc(g, i, last)
                pos = [6, 7, 8, 9, 10, 11] if not last else [6, 7, 12, 13, 14, 15]
                for n, i in enumerate(pos):
                    load_wc(g, i, last)
                    if n < 4:
                        load_wr(g, n)
                load_wr(g, 4)
                if not last:
                    for i in (12, 13):
                        load_wc(g, i, last)
                sp.wait_ge(pv_done, g * PAIRS + PAIRS)
                if not last:
                    for b in range(2):
                        load_ct(g + 1, b, ctx_t[bass.ds(g * NB + (NB + b), 1), :, :].rearrange("o p n -> (o p) n"))
                src = x[g * NB:(g + 1) * NB] if last else x[bass.ds(g * NB, NB), :, :]
                sp.dma_start(x1[:, :, :], src.rearrange("t p n -> p t n")).then_inc(x1_in, 16)
                for i in (5, 6, 7):
                    load_wr(g, i)
                if not last:
                    for b in range(2, NB):
                        load_ct(g + 1, b, ctx_t[bass.ds(g * NB + (NB + b), 1), :, :].rearrange("o p n -> (o p) n"))
                load_wr(g, 8)
                if not last:
                    for i in (14, 15):
                        load_wc(g, i, last)
                    sp.wait_ge(kv_done, g * NB + 2 * NB)
                    src = x[bass.ds(g * NB + NB, NB), :, :]
                    sp.dma_start(xn[:, :, :], src.rearrange("t p n -> p t n")).then_inc(xn_in, 16)
                with sp.Fori(0, LOOPS) as i:
                    for c in range(4):
                        for n in (16 + 2 * c, 17 + 2 * c):
                            sp.wait_ge(wc_lo, wcn(g, n, last) - 1 + i * 8)
                            sp.dma_start(wc_raw[:, n % 2, :],
                                         wc[bass.ds(i * 8 + n, 1), :, :].rearrange("o p n -> (o p) n")
                                         ).then_inc(wc_in[n % 2], 16)
                        n = 9 + c
                        sp.wait_ge(wr_lo, g * NR + n + i * 4)
                        sp.dma_start(wr_raw[:, :],
                                     wr[bass.ds(i * 4 + n, 1), :, :].rearrange("o p n -> (o p) n")
                                     ).then_inc(wr_in, 16)
                for f in range(4 * LOOPS, FT + 1):
                    for n in (16 + 2 * f, 17 + 2 * f):
                        if n < NC:
                            load_wc(g, n, last)
                        elif n > NC and not last:
                            load_wc(g + 1, n - NC - 1, False)
                    if 9 + f < NR:
                        load_wr(g, 9 + f)
                for t in range(NB):
                    sp.wait_ge(y_free, g * (CHUNKS * YN) + (4 + (CHUNKS - 1) * YN + 2 * t + 2))
                    dst = out[g * NB + t] if last else out[bass.ds(g * NB + t, 1), :, :].rearrange("o p n -> (o p) n")
                    sp.dma_start(dst, x1[:, t, :]).then_inc(stored, 16)

            sp.sem_inc(stored, 1)
            sp.dma_start(gates[:, 0:1], bass.AP(g_xattn.tensor, 0, [[0, P], [1, 1]])).then_inc(gates_in, 16)
            sp.dma_start(gates[:, 1:2], bass.AP(g_ffn.tensor, 0, [[0, P], [1, 1]])).then_inc(gates_in, 16)
            load_ct(0, 0, ctx_t[0])
            load_wc(-1, WKV, False)
            load_wc(-1, WKV + 1, False)
            load_ct(0, 1, ctx_t[1])
            sp.wait_ge(wc_lo, 1)
            sp.dma_start(wc_raw[:, 0, :], wc[WKV + 2]).then_inc(wc_in[0], 16)
            sp.wait_ge(wc_lo, 2)
            sp.dma_start(wc_raw[:, 1, :], wc[WKV + 3]).then_inc(wc_in[1], 16)
            sp.dma_start(x1[:, :, :], x[0:NB].rearrange("t p n -> p t n")).then_inc(xn_in, 16)
            load_ct(0, 2, ctx_t[2])
            load_ct(0, 3, ctx_t[3])
            load_wc(0, 0, False)
            sp.wait_ge(wc_lo, 4)
            sp.dma_start(wc_raw[:, 1, :], wc[1]).then_inc(wc_in[1], 16)
            for i in (2, 3):
                load_wc(0, i, False)
            with sp.Fori(0, NG - 1) as g:
                body(g, False)
            body(NG - 1, True)
            sp.wait_ge(stored, 16 * NB * NG + 1)

        @block.gpsimd
        def _(pool):
            nc.gpsimd.memset(mhalf[:, :], -0.5)
            nc.gpsimd.memset(ident[:, :], 0.0).then_inc(ident_zero, 1)
            pool.wait_ge(ident_zero, 1)
            nc.gpsimd.affine_select(out=ident[:, :], in_=ident[:, :], compare_op=ALU.not_equal, fill=1.0,
                                    base=0, pattern=[[-1, P]], channel_multiplier=1).then_inc(consts, 1)
            pool.wait_ge(consts, 1)

            def rsqrt(G, t, mv_ready, per, done, n):
                pool.wait_ge(mv_ready, G * NB + (t + 1))
                pool.sem_inc(passed, 1)
                nc.gpsimd.tensor_scalar(ve[:, t:t + 1], mv[:, t, 1:2], EPS, None, ALU.add).then_inc(ve_ready, 1)
                pool.wait_ge(ve_ready, per)
                nc.gpsimd.tensor_tensor(rstd[:, t:t + 1], ve[:, t:t + 1], mhalf[:, :], ALU.pow).then_inc(done, 1)

            def body(g, last):
                pool.wait_ge(xt1_done, g * 8 + 8)
                pool.wait_ge(ct_lo, g * NB + NB)
                pool.sem_inc(passed, 1)
                for buf in (kb_h, kb_l, vp_h, vp_l):
                    ins = nc.gpsimd.memset(buf[:, :, :].bitcast(F32) if buf in (kb_h, kb_l)
                                           else buf[:, :, :, :].bitcast(F32), 0.0)
                ins.then_inc(kb_zero, 1)
                for n in range(UNITS):
                    pool.wait_ge(inverted, g * UNITS + (n + 1))
                    p = pb[:, n % 4, :].rearrange("p (j k) -> p j k", j=4)
                    r = bass.AP(rinv, (n % 4) * 4, [[16, P], [1, 4], [0, P]])
                    nc.gpsimd.tensor_tensor(p, p, r, ALU.mult).then_inc(normed, 1)
                for t in range(NB):
                    rsqrt(g, t, mv2, g * (2 * NB) + (NB + t + 1), rs2, None)
                if not last:
                    for t in range(NB):
                        rsqrt(g + 1, t, mv1, g * (2 * NB) + (2 * NB + t + 1), rs1, None)

            for t in range(NB):
                rsqrt(0, t, mv1, t + 1, rs1, None)
            with pool.Fori(0, NG - 1) as g:
                body(g, False)
            body(NG - 1, True)

        @block.scalar
        def _(act):
            def copy(out, in_, scale=1.0):
                return nc.scalar.activation(out, in_, ACT.Copy, scale=scale)

            def split_wc(g, i, last, extra=0, arrived=None):
                act.wait_ge(wc_in[i % 2], wc_arrived(g, i, last) + extra)
                copy(wc_h[:, i % CS, :, :], wc_raw[:, i % 2, :].rearrange("p (k m) -> p k m", k=K8)).then_inc(wc_hi, 1)

            def split_wr(g, i, extra=0):
                act.wait_ge(wr_in, g * (16 * NR) + 16 * (i + 1) + extra)
                copy(wr_h[:, i % RS, :], wr_raw[:, :]).then_inc(wr_hi, 1)

            def split_ct(G, b):
                act.wait_ge(ct_in[b % 2], ct_arrived(G, b))
                if b >= 2:
                    act.wait_ge(kv_done, G * NB + (b - 1))
                copy(ct_h[:, b % 2, :, :], ct_raw[:, b % 2, :].rearrange("p (k m) -> p k m", k=K8)).then_inc(ct_hi, 1)

            def kv_out(G, b):
                act.wait_ge(kv_done, G * NB + (b + 1))
                if b >= 2:
                    act.wait_ge(kt_done, G * NB + (b - 1))
                copy(kn[:, b % 2, :], ps[:, b % 2, 0:2 * P]).then_inc(k_nat, 1)
                copy(vc_h[:, b, :], ps[:, b % 2, 2 * P:4 * P]).then_inc(v_hi, 1)

            def kt_out(G, b):
                act.wait_ge(kt_done, G * NB + (b + 1))
                copy(kc_h[:, :, b * P:(b + 1) * P],
                     ps[:, 2 + b % 2, 0:2 * P].rearrange("p (a m) -> p a m", a=2)).then_inc(k_hi, 1)

            def xt_out(G, t, h, done, hi, bank):
                act.wait_ge(done, G * 8 + (2 * t + h + 1))
                copy(xt_h[:, 4 * h:4 * h + 4, t * P:(t + 1) * P],
                     ps[:, bank, :].rearrange("p (k m) -> p k m", k=4)).then_inc(hi, 1)

            def q_out(g, i):
                act.wait_ge(wc_used, used(g, i))
                copy(qo_h[:, i, :], ps[:, 6 + i % 2, :], SCALE).then_inc(q_hi, 1)

            def pt_out(g, n):
                m, gi = n // 2, n % 2
                act.wait_ge(pt_done, g * UNITS + (n + 1))
                if m >= 2:
                    act.wait_ge(pv_done, g * PAIRS + (m - 1))
                copy(pt_h[:, m % 2, :, gi * P:(gi + 1) * P],
                     ps[:, 3 + n % 2, :].rearrange("p (j q) -> p j q", j=4)).then_inc(pt_hi, 1)

            def exps(g, n):
                act.wait_ge(maxed, g * UNITS + (n + 1))
                if n >= 4:
                    act.wait_ge(pt_done, g * UNITS + (n - 3))
                for j in range(4):
                    ins = nc.scalar.activation(pb[:, n % 4, j * P:(j + 1) * P], ps[:, n % 3, j * P:(j + 1) * P],
                                               ACT.Exp, bias=nmx[:, n % 4, j:j + 1],
                                               accum_out=psum_[:, n % 4, j:j + 1])
                ins.then_inc(exped, 1)

            def o_out(g, m):
                k, b = m // NB, m % NB
                act.wait_ge(pv_done, g * PAIRS + (m + 1))
                copy(qo_h[:, 2 * k:2 * k + 2, b * P:(b + 1) * P],
                     ps[:, 5, 0:2 * P].rearrange("p (g q) -> p g q", g=2)).then_inc(o_hi, 1)

            def hidden(g, f, fi, iw, last, splits, tail=False):
                s = f % 2
                rows = P if not tail else FR
                act.wait_ge(wc_used, used(g, iw[0]) + fi * 8)
                if tail:
                    act.wait_ge(up_free, g * (FT + 1) + (FT + 2))
                else:
                    act.wait_ge(up_free, g * (FT + 1) + (f + 1) + fi * 4)
                if tail:
                    nc.scalar.activation(sg[0:FR, s, :], ps[0:FR, 2, :], ACT.Silu)
                    copy(sg[0:FR, 0, :], ps[FR:P, 2, :]).then_inc(gate_free, 1)
                else:
                    nc.scalar.activation(sg[:, s, :], ps[:, 2 * s, :], ACT.Silu).then_inc(gate_free, 1)
                splits()
                act.wait_ge(up_free, g * (FT + 1) + (f + 3) + fi * 4)
                copy(h_h[0:rows, f % 4, :], hf[0:rows, s, :]).then_inc(h_hi, 1)

            def body(g, last):
                def split_next(i):
                    j = i + 4 if (not last or i < 4) else i + 8
                    split_wc(g, j, last)

                for i in (0, 1):
                    q_out(g, i)
                    split_next(i)
                act.wait_ge(stored, g * (16 * NB) + 1)
                for n in range(STEPS + 1):
                    if n >= 5 and n % 2 == 1:
                        o_out(g, (n - 5) // 2)
                    if 2 <= n < UNITS + 2:
                        pt_out(g, n - 2)
                    if n < UNITS:
                        exps(g, n)
                    k = n // 8
                    if n % 8 == 4 and k < 3:
                        q_out(g, 2 * k + 2)
                        split_next(2 * k + 2)
                    if n % 8 == 7 and k < 3:
                        q_out(g, 2 * k + 3)
                        split_next(2 * k + 3)
                    if n in (2, 6, 10, 14):
                        split_wr(g, n // 4)
                for e in range(4):
                    act.wait_ge(o_first, g * 4 + (e + 1))
                    split_wr(g, 4 + e)
                    if e < 2 and not last:
                        split_ct(g + 1, e)
                G = g + 1
                if not last:
                    kv_out(G, 0)
                    split_ct(G, 2)
                    kv_out(G, 1)
                    split_ct(G, 3)
                    kt_out(G, 0)
                for t in range(NB):
                    for h in range(2):
                        if t == NB - 1 and h == 0 and not last:
                            for i in range(WFF, WFF + 4):
                                act.wait_ge(kv_done, g * NB + 2 * NB)
                                split_wc(g, i, last)
                            kt_out(G, 3)
                        xt_out(g, t, h, xt2_done, xt2_hi, 4 + 2 * (t % 2) + h)
                    if t < 2 and not last:
                        kv_out(G, t + 2)
                        kt_out(G, t + 1)
                with act.Fori(0, LOOPS) as i:
                    for c in range(4):
                        def splits(c=c):
                            split_wc(g, 16 + 2 * c, last, i * 64)
                            act.wait_ge(wc_used, used(g, 13 + 2 * c) + i * 8)
                            split_wc(g, 17 + 2 * c, last, i * 64)
                            split_wr(g, 8 + c, i * 64)
                        hidden(g, c, i, (WFF + 2 * c,), last, splits)
                for f in range(4 * LOOPS, FT + 1):
                    def splits(f=f):
                        for u in range(2):
                            n = 16 + 2 * f + u
                            if u and f < FT:
                                act.wait_ge(wc_used, used(g, 13 + 2 * f))
                            if n < NC:
                                split_wc(g, n, last)
                            elif n > NC and not last:
                                split_wc(g + 1, n - NC - 1, False)
                        split_wr(g, 8 + f)
                    hidden(g, f, 0, (WFF + 2 * f,), last, splits, tail=f == FT)
                if not last:
                    for t in range(NB):
                        for h in range(2):
                            xt_out(G, t, h, xt1_done, xt1_hi, (3, 0, 1, 2)[(2 * t + h) % 4])

            act.wait_ge(gates_in, 32)
            nc.scalar.activation(tg[:, :], gates[:, :], ACT.Tanh).then_inc(tg_ready, 1)
            act.wait_ge(tg_ready, 1)
            copy(tg[:, :], tg[:, :]).then_inc(gate_free, 2)
            split_ct(0, 0)
            for i in range(2):
                act.wait_ge(wc_in[i], 16)
                copy(wc_h[:, i, :, :], wc_raw[:, i, :].rearrange("p (k m) -> p k m", k=K8)).then_inc(wc_hi, 1)
            split_ct(0, 1)
            for i in range(2):
                act.wait_ge(wc_in[i], 32)
                copy(wc_h[:, 2 + i, :, :], wc_raw[:, i, :].rearrange("p (k m) -> p k m", k=K8)).then_inc(wc_hi, 1)
            kv_out(0, 0)
            split_ct(0, 2)
            kv_out(0, 1)
            split_ct(0, 3)
            kt_out(0, 0)
            for t in range(NB):
                for h in range(2):
                    if t == NB - 1 and h == 0:
                        for i in range(4):
                            act.wait_ge(kv_done, NB)
                            split_wc(0, i, False)
                        kt_out(0, 3)
                    xt_out(0, t, h, xt1_done, xt1_hi, 4 + 2 * (t % 2) + h)
                if t < 2:
                    kv_out(0, t + 2)
                    kt_out(0, t + 1)
            with act.Fori(0, NG - 1) as g:
                body(g, False)
            body(NG - 1, True)

        @block.vector
        def _(dve):
            def minus(out, whole, hi):
                return nc.vector.tensor_tensor(out, whole, hi.bitcast(F32), ALU.subtract)

            def split_wc(g, i, last, extra=0):
                dve.wait_ge(wc_hi, wcn(g, i, last) + 1 + extra)
                minus(wc_l[:, i % CS, :, :], wc_raw[:, i % 2, :].rearrange("p (k m) -> p k m", k=K8),
                      wc_h[:, i % CS, :, :]).then_inc(wc_lo, 1)

            def split_wr(g, i, extra=0):
                dve.wait_ge(wr_hi, g * NR + (i + 1) + extra)
                minus(wr_l[:, i % RS, :], wr_raw[:, :], wr_h[:, i % RS, :]).then_inc(wr_lo, 1)

            def split_ct(G, b):
                dve.wait_ge(ct_hi, G * NB + (b + 1))
                minus(ct_l[:, b % 2, :, :], ct_raw[:, b % 2, :].rearrange("p (k m) -> p k m", k=K8),
                      ct_h[:, b % 2, :, :]).then_inc(ct_lo, 1)

            def v_out(G, b):
                dve.wait_ge(v_hi, G * NB + (b + 1))
                minus(vc_l[:, b, :], ps[:, b % 2, 2 * P:4 * P], vc_h[:, b, :]).then_inc(v_lo, 1)

            def k_out(G, b):
                dve.wait_ge(k_hi, G * NB + (b + 1))
                minus(kc_l[:, :, b * P:(b + 1) * P], ps[:, 2 + b % 2, 0:2 * P].rearrange("p (a m) -> p a m", a=2),
                      kc_h[:, :, b * P:(b + 1) * P]).then_inc(k_lo, 1)

            def xt_out(G, t, h, hi, lo, bank):
                dve.wait_ge(hi, G * 8 + (2 * t + h + 1))
                where = (slice(None), slice(4 * h, 4 * h + 4), slice(t * P, (t + 1) * P))
                minus(xt_l[where], ps[:, bank, :].rearrange("p (k m) -> p k m", k=4), xt_h[where]).then_inc(lo, 1)

            def q_out(g, i):
                dve.wait_ge(q_hi, g * NQ + (i + 1))
                nc.vector.scalar_tensor_tensor(qo_l[:, i, :], ps[:, 6 + i % 2, :], SCALE, qo_h[:, i, :].bitcast(F32),
                                               ALU.mult, ALU.subtract).then_inc(q_lo, 1)

            def build_kb(g, a, b):
                for kb, kc in ((kb_h, kc_h), (kb_l, kc_l)):
                    for j in range(4):
                        rows = slice(j * HD, (j + 1) * HD)
                        ins = nc.vector.tensor_copy(kb[rows, b, j * P:(j + 1) * P],
                                                    kc[rows, a, b * P:(b + 1) * P].bitcast(F32))
                ins.then_inc(kb_built, 1)

            def build_vp(g, m):
                a, b = m // NB // 2, m % NB
                for vp, vc in ((vp_h, vc_h), (vp_l, vc_l)):
                    dst = bass.AP(vp, (m % 2) * 4 * P, [[8 * P, P], [P + HD, 4], [1, HD]])
                    ins = nc.vector.tensor_copy(dst, vc[:, b, a * P:(a + 1) * P].rearrange("p (j d) -> p j d", j=4).bitcast(F32))
                ins.then_inc(vp_built, 1)

            def row_max(g, n):
                dve.wait_ge(s_done, g * UNITS + (n + 1))
                nc.vector.tensor_reduce(nmx[:, n % 4, :], ps[:, n % 3, :].rearrange("p (j k) -> p j k", j=4),
                                        AX_X, ALU.max, negate=True).then_inc(maxed, 1)

            def invert(g, n):
                dve.wait_ge(exped, g * UNITS + (n + 1))
                nc.vector.reciprocal(rinv[:, n % 4, :], psum_[:, n % 4, :]).then_inc(inverted, 1)

            def pt_out(g, n):
                m, gi = n // 2, n % 2
                dve.wait_ge(pt_hi, g * UNITS + (n + 1))
                where = (slice(None), m % 2, slice(None), slice(gi * P, (gi + 1) * P))
                minus(pt_l[where], ps[:, 3 + n % 2, :].rearrange("p (j q) -> p j q", j=4), pt_h[where]).then_inc(pt_lo, 1)

            def o_out(g, m):
                k, b = m // NB, m % NB
                dve.wait_ge(o_hi, g * PAIRS + (m + 1))
                where = (slice(None), slice(2 * k, 2 * k + 2), slice(b * P, (b + 1) * P))
                minus(qo_l[where], ps[:, 5, 0:2 * P].rearrange("p (g q) -> p g q", g=2), qo_h[where]).then_inc(o_lo, 1)

            def stats(G, t, src, counted, done):
                for h in range(2):
                    ins = nc.vector.bn_stats(st[:, t % 2, 6 * h:6 * h + 6], src[:, t, h * HALF:(h + 1) * HALF])
                ins.then_inc(counted, 1)
                dve.wait_ge(counted, G * NB + (t + 1))
                dve.sem_inc(passed, 1)
                nc.vector.bn_aggr(mv[:, t, :], st[:, t % 2, :]).then_inc(done, 1)

            def normalise(G, t, dst, src, rs, done):
                dve.wait_ge(rs, G * NB + (t + 1))
                nc.vector.tensor_scalar(dst, src, mv[:, t, 0:1], rstd[:, t:t + 1],
                                        ALU.subtract, ALU.mult).then_inc(done, 1)

            def hidden(g, f, fi, last, splits, tail=False):
                s = f % 2
                rows = P if not tail else FR
                dve.wait_ge(gate_free, g * (FT + 1) + (f + 3) + fi * 4)
                if tail:
                    nc.vector.tensor_tensor(hf[0:FR, s, :], sg[0:FR, s, :], sg[0:FR, 0, :], ALU.mult).then_inc(up_free, 1)
                else:
                    dve.wait_ge(wc_used, used(g, WFF + 1 + 2 * f) + fi * 8)
                    nc.vector.tensor_tensor(hf[:, s, :], sg[:, s, :], ps[:, 2 * s + 1, :], ALU.mult).then_inc(up_free, 1)
                splits()
                dve.wait_ge(h_hi, g * (FT + 1) + (f + 1) + fi * 4)
                minus(h_l[0:rows, f % 4, :], hf[0:rows, s, :], h_h[0:rows, f % 4, :]).then_inc(h_lo, 1)

            def add_y(g, c, fi):
                for idx in range(YN):
                    t, d = idx // NH, idx % NH
                    dve.wait_ge(y_done, g * (CHUNKS * YN) + (c * YN + idx + 1) + fi * (2 * YN))
                    place = x1[:, t, d * HALF:(d + 1) * HALF]
                    nc.vector.scalar_tensor_tensor(place, ps[:, 4 + idx % 4, :], tg[:, 1:2], place,
                                                   ALU.mult, ALU.add).then_inc(y_free, 1)

            def body(g, last):
                def split_next(i):
                    j = i + 4 if (not last or i < 4) else i + 8
                    split_wc(g, j, last)

                dve.wait_ge(kb_zero, g + 1)
                dve.wait_ge(k_lo, g * NB + NB)
                dve.wait_ge(v_lo, g * NB + NB)
                for b in range(NB):
                    build_kb(g, 0, b)
                build_vp(g, 0)
                build_vp(g, 1)
                for i in (0, 1):
                    q_out(g, i)
                    split_next(i)
                for n in range(STEPS + 1):
                    if n < UNITS:
                        row_max(g, n)
                    if n >= 5 and n % 2 == 1:
                        m = (n - 5) // 2
                        o_out(g, m)
                        if m + 2 < PAIRS:
                            build_vp(g, m + 2)
                    if 2 <= n < UNITS + 2:
                        pt_out(g, n - 2)
                    if n >= 11 and n % 2 == 1 and n <= 17:
                        b = (n - 11) // 2
                        dve.wait_ge(s_done, g * UNITS + (8 + 2 * b + 2))
                        build_kb(g, 1, b)
                    if n < UNITS:
                        invert(g, n)
                    k = n // 8
                    if n % 8 == 4 and k < 3:
                        q_out(g, 2 * k + 2)
                        split_next(2 * k + 2)
                    if n % 8 == 7 and k < 3:
                        q_out(g, 2 * k + 3)
                        split_next(2 * k + 3)
                    if n in (2, 6, 10, 14):
                        split_wr(g, n // 4)
                for e in range(4):
                    split_wr(g, 4 + e)
                    if e < 2 and not last:
                        split_ct(g + 1, e)
                G = g + 1
                dve.wait_ge(x1_in, g * 16 + 16)
                for t in range(NB):
                    dve.wait_ge(o_done, g * NB + (t + 1))
                    for d in range(NH):
                        place = x1[:, t, d * HALF:(d + 1) * HALF]
                        nc.vector.scalar_tensor_tensor(place, ps[:, 2 * t + d, :], tg[:, 0:1], place,
                                                       ALU.mult, ALU.add).then_inc(x1_add, 1)
                    dve.wait_ge(x1_add, g * YN + (2 * t + 2))
                    stats(g, t, x1, st2, mv2)
                    if t < 2:
                        normalise(g, t, xn2[:, t % 2, :], x1[:, t, :], rs2, xn2_ready)
                if not last:
                    v_out(G, 0)
                    split_ct(G, 2)
                    v_out(G, 1)
                    split_ct(G, 3)
                    k_out(G, 0)
                for t in range(NB):
                    for h in range(2):
                        if t == NB - 1 and h == 0 and not last:
                            for i in range(WFF, WFF + 4):
                                split_wc(g, i, last)
                            k_out(G, 3)
                        xt_out(g, t, h, xt2_hi, xt2_lo, 4 + 2 * (t % 2) + h)
                    if t < 2:
                        normalise(g, t + 2, xn2[:, t % 2, :], x1[:, t + 2, :], rs2, xn2_ready)
                        if not last:
                            v_out(G, t + 2)
                            k_out(G, t + 1)
                with dve.Fori(0, LOOPS) as i:
                    for c in range(4):
                        def splits(c=c):
                            split_wc(g, 16 + 2 * c, last, i * 8)
                            split_wc(g, 17 + 2 * c, last, i * 8)
                            split_wr(g, 8 + c, i * 4)
                        hidden(g, c, i, last, splits)
                    add_y(g, 0, i)
                    add_y(g, 1, i)
                for f in range(4 * LOOPS, FT + 1):
                    t = f - 4 * LOOPS
                    if t < NB and not last:
                        if t == 0:
                            dve.wait_ge(xn_in, g * 16 + 32)
                        stats(G, t, xn, st1, mv1)

                    def splits(f=f):
                        for u in range(2):
                            n = 16 + 2 * f + u
                            if n < NC:
                                split_wc(g, n, last)
                            elif n > NC and not last:
                                split_wc(g + 1, n - NC - 1, False)
                        split_wr(g, 8 + f)
                    hidden(g, f, 0, last, splits, tail=f == FT)
                    if t < NB and not last:
                        normalise(G, t, xn[:, t, :], xn[:, t, :], rs1, xn1_ready)
                    if t == 3:
                        add_y(g, 8, 0)
                        add_y(g, 9, 0)
                if not last:
                    for t in range(NB):
                        for h in range(2):
                            xt_out(G, t, h, xt1_hi, xt1_lo, (3, 0, 1, 2)[(2 * t + h) % 4])
                add_y(g, 10, 0)

            nc.vector.memset(st[:, 0, :], 0.0).then_inc(up_free, 2)
            nc.vector.memset(st[:, 1, :], 0.0).then_inc(y_free, 4)
            dve.wait_ge(up_free, 2)
            dve.wait_ge(y_free, 4)
            dve.wait_ge(gate_free, 2)
            split_ct(0, 0)
            for i in range(2):
                dve.wait_ge(wc_hi, i + 1)
                minus(wc_l[:, i, :, :], wc_raw[:, i, :].rearrange("p (k m) -> p k m", k=K8), wc_h[:, i, :, :]).then_inc(wc_lo, 1)
            split_ct(0, 1)
            for i in range(2):
                dve.wait_ge(wc_hi, i + 3)
                minus(wc_l[:, 2 + i, :, :], wc_raw[:, i, :].rearrange("p (k m) -> p k m", k=K8), wc_h[:, 2 + i, :, :]).then_inc(wc_lo, 1)
            dve.wait_ge(xn_in, 16)
            for t in range(NB):
                stats(0, t, x1, st1, mv1)
                if t > 0:
                    normalise(0, t - 1, x1[:, t - 1, :], x1[:, t - 1, :], rs1, xn1_ready)
            v_out(0, 0)
            split_ct(0, 2)
            v_out(0, 1)
            split_ct(0, 3)
            k_out(0, 0)
            normalise(0, 3, x1[:, 3, :], x1[:, 3, :], rs1, xn1_ready)
            for t in range(NB):
                for h in range(2):
                    if t == NB - 1 and h == 0:
                        for i in range(4):
                            split_wc(0, i, False)
                        k_out(0, 3)
                    xt_out(0, t, h, xt1_hi, xt1_lo, 4 + 2 * (t % 2) + h)
                if t < 2:
                    v_out(0, t + 2)
                    k_out(0, t + 1)
            with dve.Fori(0, NG - 1) as g:
                body(g, False)
            body(NG - 1, True)

        @block.tensor
        def _(pe):
            def three(out, w_h, w_l, m_h, m_l, first, last):
                pe.matmul(out, w_h, m_h, start=first, stop=False)
                pe.matmul(out, w_h, m_l, start=False, stop=False)
                return pe.matmul(out, w_l, m_h, start=False, stop=last)

            def column_tile(out, i, ks):
                s = i % CS
                for k in ks:
                    ins = three(out, wc_h[:, s, k, :], wc_l[:, s, k, :], xt_h[:, k, :], xt_l[:, k, :],
                                k == 0, k == K8 - 1)
                return ins

            def q_tile(g, i, ks):
                if ks[0] == 0:
                    pe.wait_ge(wc_lo, wcn(g, i, False) + 1)
                    if i >= 2:
                        pe.wait_ge(q_lo, g * NQ + (i - 1))
                ins = column_tile(ps[:, 6 + i % 2, :], i, ks)
                if ks[-1] == K8 - 1:
                    ins.then_inc(wc_used, 1)

            def scores(g, n):
                k, b, gi = n // 8, n % 8 // 2, n % 2
                a, iq = k // 2, 2 * k + gi
                pe.wait_ge(q_lo, g * NQ + (iq + 1))
                pe.wait_ge(kb_built, g * (2 * NB) + (a * NB + b + 1))
                if n >= 3:
                    pe.wait_ge(exped, g * UNITS + (n - 2))
                toks = slice(b * P, (b + 1) * P)
                three(ps[:, n % 3, :], qo_h[:, iq, toks], qo_l[:, iq, toks], kb_h[:, b, :], kb_l[:, b, :],
                      True, True).then_inc(s_done, 1)

            def transpose_p(g, n):
                pe.wait_ge(normed, g * UNITS + (n + 1))
                if n >= 2:
                    pe.wait_ge(pt_lo, g * UNITS + (n - 1))
                for j in range(4):
                    ins = pe.transpose(ps[:, 3 + n % 2, j * P:(j + 1) * P], pb[:, n % 4, j * P:(j + 1) * P], ident[:, :])
                ins.then_inc(pt_done, 1)

            def weigh_values(g, m):
                pe.wait_ge(pt_lo, g * UNITS + (2 * m + 2))
                pe.wait_ge(vp_built, g * PAIRS + (m + 1))
                if m >= 1:
                    pe.wait_ge(o_lo, g * PAIRS + m)
                for j in range(4):
                    ins = three(ps[:, 5, 0:2 * P], vp_h[:, m % 2, j, :], vp_l[:, m % 2, j, :],
                                pt_h[:, m % 2, j, :], pt_l[:, m % 2, j, :], j == 0, j == 3)
                ins.then_inc(pv_done, 1)

            def o_part(e, t, d):
                toks, cols = slice(t * P, (t + 1) * P), slice(d * HALF, (d + 1) * HALF)
                return three(ps[:, 2 * t + d, :], qo_h[:, e, toks], qo_l[:, e, toks],
                             wr_h[:, e % RS, cols], wr_l[:, e % RS, cols], e == 0, e == NO - 1)

            def kv(G, b):
                pe.wait_ge(ct_lo, G * NB + (b + 1))
                if b >= 2:
                    pe.wait_ge(v_lo, G * NB + (b - 1))
                for k in range(K8):
                    ins = three(ps[:, b % 2, :].rearrange("p (s m) -> p s m", s=CS),
                                ct_h[:, b % 2, k, :], ct_l[:, b % 2, k, :], wc_h[:, :, k, :], wc_l[:, :, k, :],
                                k == 0, k == K8 - 1)
                ins.then_inc(kv_done, 1)

            def kt(G, b):
                pe.wait_ge(k_nat, G * NB + (b + 1))
                if b >= 2:
                    pe.wait_ge(k_lo, G * NB + (b - 1))
                for a in range(2):
                    ins = pe.transpose(ps[:, 2 + b % 2, a * P:(a + 1) * P], kn[:, b % 2, a * P:(a + 1) * P], ident[:, :])
                ins.then_inc(kt_done, 1)

            def xt(src, h, bank, done):
                for c in range(4):
                    k = 4 * h + c
                    ins = pe.transpose(ps[:, bank, c * P:(c + 1) * P], src[:, k * P:(k + 1) * P], ident[:, :])
                ins.then_inc(done, 1)

            def gate_up(g, f, fi, last):
                s = f % 2
                for u in range(2):
                    i = WFF + 2 * f + u
                    pe.wait_ge(wc_lo, wcn(g, i, last) + 1 + fi * 8)
                    pe.wait_ge(up_free if u else gate_free, g * (FT + 1) + (f + 1) + fi * 4)
                    column_tile(ps[:, 2 * s + u, :], i, range(K8)).then_inc(wc_used, 1)

            def down(g, c, fi):
                rows = [P, FR if c == CHUNKS - 1 else P]
                pe.wait_ge(wr_lo, g * NR + (NO + 2 * c + 2) + fi * 4)
                pe.wait_ge(h_lo, g * (FT + 1) + (2 * c + 2) + fi * 4)
                for idx in range(YN):
                    t, d = idx // NH, idx % NH
                    toks, cols = slice(t * P, (t + 1) * P), slice(d * HALF, (d + 1) * HALF)
                    pe.wait_ge(y_free, g * (CHUNKS * YN) + (c * YN + idx + 1) + fi * (2 * YN))
                    for u in range(2):
                        s, r = (2 * c + u) % 4, rows[u]
                        ins = three(ps[:, 4 + idx % 4, :], h_h[0:r, s, toks], h_l[0:r, s, toks],
                                    wr_h[0:r, s, cols], wr_l[0:r, s, cols], u == 0, u == 1)
                    ins.then_inc(y_done, 1)

            def body(g, last):
                pe.wait_ge(xt1_lo, g * 8 + 8)
                pe.wait_ge(y_free, g * (CHUNKS * YN) + 4)
                for i in (0, 1):
                    q_tile(g, i, range(K8))
                for n in range(STEPS):
                    k, r = n // 8, n % 8
                    if k < 3 and r < 7:
                        lo, hi = r * 16 // 7, (r + 1) * 16 // 7
                        for i in range(2):
                            ks = [w - 8 * i for w in range(lo, hi) if w // 8 == i]
                            if ks:
                                q_tile(g, 2 * k + 2 + i, ks)
                    if n < UNITS:
                        scores(g, n)
                    if 2 <= n < UNITS + 2:
                        transpose_p(g, n - 2)
                    if n >= 4 and n % 2 == 0:
                        weigh_values(g, (n - 4) // 2)
                pe.wait_ge(o_lo, g * PAIRS + PAIRS)
                pe.wait_ge(wr_lo, g * NR + 4)
                for e in range(4):
                    for t in range(NB):
                        for d in range(NH):
                            ins = o_part(e, t, d)
                    ins.then_inc(o_first, 1)
                for t in range(NB):
                    for e in range(4, NO):
                        if t == 0:
                            pe.wait_ge(wr_lo, g * NR + (e + 1))
                        for d in range(NH):
                            ins = o_part(e, t, d)
                    ins.then_inc(o_done, 1)
                G = g + 1

                def xt2(t):
                    pe.wait_ge(xn2_ready, g * NB + (t + 1))
                    for h in range(2):
                        if t < 2:
                            pe.wait_ge(x1_add, g * YN + (6 + 2 * t))
                        else:
                            pe.wait_ge(xt2_lo, g * 8 + (2 * (t - 2) + h + 1))
                        xt(xn2[:, t % 2, :], h, 4 + 2 * (t % 2) + h, xt2_done)
                if not last:
                    pe.wait_ge(wc_lo, wcn(g, WKV + 3, False) + 1)
                    pe.wait_ge(x1_add, g * YN + 2)
                    kv(G, 0)
                    kv(G, 1)
                    pe.wait_ge(x1_add, g * YN + 4)
                    kt(G, 0)
                    xt2(0)
                    kv(G, 2)
                    kt(G, 1)
                    xt2(1)
                    kv(G, 3)
                    kt(G, 2)
                    xt2(2)
                    kt(G, 3)
                    xt2(3)
                    pe.wait_ge(v_lo, g * NB + 2 * NB)
                    pe.wait_ge(k_lo, g * NB + 2 * NB)
                else:
                    for t in range(NB):
                        xt2(t)
                pe.wait_ge(xt2_lo, g * 8 + 8)
                pe.sem_inc(passed, 1)
                with pe.Fori(0, LOOPS) as i:
                    for c in range(4):
                        gate_up(g, c, i, last)
                    down(g, 0, i)
                    down(g, 1, i)
                for f in range(4 * LOOPS, 4 * LOOPS + 4):
                    gate_up(g, f, 0, last)
                down(g, 8, 0)
                down(g, 9, 0)
                gate_up(g, FT - 1, 0, last)
                pe.wait_ge(wc_lo, wcn(g, WMIX, last) + 1)
                pe.wait_ge(gate_free, g * (FT + 1) + (FT + 1))
                column_tile(ps[:, 2, :], WMIX, range(K8)).then_inc(wc_used, 1)
                if not last:
                    for t in range(NB):
                        pe.wait_ge(xn1_ready, g * NB + (NB + t + 1))
                        for h in range(2):
                            q = 2 * t + h
                            if q == 0:
                                pe.wait_ge(up_free, g * (FT + 1) + (FT + 1))
                            elif q == 1:
                                pe.wait_ge(gate_free, g * (FT + 1) + (FT + 2))
                            elif q == 2:
                                pe.wait_ge(up_free, g * (FT + 1) + (FT + 2))
                            elif q == 3:
                                pe.wait_ge(gate_free, g * (FT + 1) + (FT + 3))
                            else:
                                pe.wait_ge(xt1_lo, g * 8 + (8 + q - 3))
                            xt(xn[:, t, :], h, (3, 0, 1, 2)[q % 4], xt1_done)
                down(g, CHUNKS - 1, 0)

            def xt1_first(t):
                pe.wait_ge(xn1_ready, t + 1)
                for h in range(2):
                    if t >= 2:
                        pe.wait_ge(xt1_lo, 2 * (t - 2) + h + 1)
                    xt(x1[:, t, :], h, 4 + 2 * (t % 2) + h, xt1_done)

            pe.wait_ge(consts, 1)
            pe.wait_ge(wc_lo, NKV)
            kv(0, 0)
            kv(0, 1)
            kt(0, 0)
            xt1_first(0)
            kv(0, 2)
            kt(0, 1)
            xt1_first(1)
            kv(0, 3)
            kt(0, 2)
            xt1_first(2)
            kt(0, 3)
            xt1_first(3)
            with pe.Fori(0, NG - 1) as g:
                body(g, False)
            body(NG - 1, True)


def kernel(x, ctx_4096, g_xattn, g_ffn, L0_xattn_Wq, L0_xattn_Wk, L0_xattn_Wv, L0_xattn_Wo,
           L0_ffn_W_gate, L0_ffn_W_up, L0_ffn_W_down):
    import numpy as np
    import concourse.bacc as bacc
    from concourse.bass_utils import run_bass_kernel_spmd

    def columns(w):
        n = w.shape[1] // P
        return w.reshape(K8, P, n, P).transpose(2, 1, 0, 3).reshape(n, P, K8 * P)

    def heads(w):
        return w.reshape(D, 2, 4, GQ, HD).transpose(0, 1, 3, 2, 4).reshape(D, D)

    wq, wk, wv, wo = (np.asarray(w) for w in (L0_xattn_Wq, L0_xattn_Wk, L0_xattn_Wv, L0_xattn_Wo))
    wg, wu, wd = np.asarray(L0_ffn_W_gate).T, np.asarray(L0_ffn_W_up).T, np.asarray(L0_ffn_W_down).T
    g_tiles, u_tiles = columns(wg[:, :FT * P]), columns(wu[:, :FT * P])
    ffn = np.stack([g_tiles, u_tiles], axis=1).reshape(2 * FT, P, K8 * P)
    mix = columns(np.concatenate([wg[:, FT * P:], wu[:, FT * P:]], axis=1))
    wc = np.concatenate([columns(heads(wq)), columns(np.concatenate([wk, wv], axis=1)), ffn, mix], axis=0)
    wo_rows = heads(wo.T).T.reshape(NO, P, D)
    wd_rows = np.concatenate([wd, np.zeros((P - FR, D), wd.dtype)], axis=0).reshape(FT + 1, P, D)
    wr = np.concatenate([wo_rows, wd_rows], axis=0)
    ctx_t = np.asarray(ctx_4096).reshape(BATCH, SEQ, K8, P).transpose(0, 3, 2, 1).reshape(BATCH, P, K8 * SEQ)

    nc = bacc.Bacc("TRN2", target_bir_lowering=False, num_devices=1)
    given = {"x": np.asarray(x), "ctx_t": ctx_t, "wc": wc, "wr": wr,
             "g_xattn": np.asarray(g_xattn), "g_ffn": np.asarray(g_ffn)}
    arrays, args = {}, []
    for name, a in given.items():
        a = np.ascontiguousarray(a)
        arrays[f"in_{name}"] = a
        args.append(nc.dram_tensor(f"in_{name}", a.shape, mybir.dt.from_np(a.dtype), kind="ExternalInput").ap())
    out = nc.dram_tensor("out", (BATCH, SEQ, D), F32, kind="ExternalOutput").ap()
    gated_cross_attention_ffn(nc, *args, out)
    r = run_bass_kernel_spmd(nc, [arrays], core_ids=[0])
    return r.results[0]["out"]
```

```python
from contextlib import ExitStack

import concourse.bass as bass
from concourse import mybir

P = 128
BATCH, SEQ, D = 16, 128, 1024
HEADS, KV_HEADS, HD = 32, 8, 32
GQ = HEADS // KV_HEADS
F = 2752
EPS = 1e-5
SCALE = float(HD) ** -0.5

TOK = 512
NB = TOK // SEQ
NG = BATCH // NB
K8 = D // P
HALF = 512
NH = D // HALF

NQ = D // P
NKV = 2 * KV_HEADS * HD // P
FT = -(-F // P)
FR = F % P
MIX = FT - 2
NC = NQ + NKV + 2 * FT - 1
WKV, WFF = NQ, NQ + NKV
CS = 4
NO = D // P
NR = NO + FT
RS = 4

UNITS = NB * NH * GQ
PAIRS = UNITS // 2
H2 = P // 2
TR_BANKS = (1, 0, 2, 3)
CHUNKS = FT // 2
YN = NB * NH
LOOPS = 4
STEPS = UNITS + 5
COL_STEP = {5: 0, 6: 5, 7: 9, 8: 32, 9: 33}
ROW_STEP = {0: 1, 1: 13, 2: 17, 3: 21}
KB_STEPS = (12, 13, 17, 20)


def q_bank(i):
    return 4 * i if i < 2 else 6 + i % 2


def gate_tile(f):
    return WFF + 2 * f - (1 if f > MIX else 0)


def extra_slot(i):
    if i < 2:
        return i
    return (i - WFF) % 8 if i >= WFF and (i - WFF) % 8 < 2 else None


F32 = mybir.dt.float32
F32R = mybir.dt.float32r
ACT = mybir.ActivationFunctionType
ALU = mybir.AluOpType
AX_X = mybir.AxisListType.X


def gated_cross_attention_ffn(nc, x, ctx_t, wc, wr, g_xattn, g_ffn, out):
    with ExitStack() as ctx:
        end = [(nc.sbuf_base + 31) // 32 * 32]

        def at(name, shape, dt, offset):
            return nc.alloc_sbuf_tensor_at(name, shape, dt, offset=offset)

        def sb(name, shape, dt=F32):
            size = 4
            for n in shape[1:]:
                size *= n
            offset = end[0]
            end[0] += (size + 31) // 32 * 32
            return at(name, shape, dt, offset), offset

        xt_h, _ = sb("xt_h", [P, K8, TOK], F32R)
        xt_l, o_xl = sb("xt_l", [P, K8, TOK], F32R)
        kv_raw = at("kv_raw", [P, NKV, K8 * P], F32, o_xl)
        wc_h, _ = sb("wc_h", [P, CS, K8, P], F32R)
        wc_l, _ = sb("wc_l", [P, CS, K8, P], F32R)
        wc_raw, _ = sb("wc_raw", [P, 2, K8 * P])
        wr_h, _ = sb("wr_h", [P, RS, D], F32R)
        wr_l, _ = sb("wr_l", [P, RS, D], F32R)
        wr_raw, _ = sb("wr_raw", [P, D])
        kc_h, _ = sb("kc_h", [P, 2, TOK], F32R)
        kc_l, _ = sb("kc_l", [P, 2, TOK], F32R)
        vc_h, _ = sb("vc_h", [P, NB, 2 * P], F32R)
        vc_l, _ = sb("vc_l", [P, NB, 2 * P], F32R)
        qo_h, o_qh = sb("qo_h", [P, 2 * GQ, TOK], F32R)
        qo_l, o_ql = sb("qo_l", [P, 2 * GQ, TOK], F32R)
        h_h = at("h_h", [P, 4, TOK], F32R, o_qh)
        h_l = at("h_l", [P, 4, TOK], F32R, o_ql)
        wx_h = at("wx_h", [P, 2, K8, P], F32R, o_qh + 4 * TOK * 4)
        wx_l = at("wx_l", [P, 2, K8, P], F32R, o_ql + 4 * TOK * 4)
        x1, o_x1 = sb("x1", [P, NB, D])
        pt_h = at("pt_h", [P, 2, 4, 2 * P], F32R, o_x1)
        pt_l = at("pt_l", [P, 2, 4, 2 * P], F32R, o_x1 + 8192)
        xn, o_kb = sb("xn", [P, NB, D])
        kb_h = at("kb_h", [P, NB, HALF], F32R, o_kb)
        kb_l = at("kb_l", [P, NB, HALF], F32R, o_kb + 8192)
        ct_h = at("ct_h", [P, 2, K8, P], F32R, o_kb)
        ct_l = at("ct_l", [P, 2, K8, P], F32R, o_kb + 8192)
        ct_raw, o_vp = sb("ct_raw", [P, 2, K8 * P])
        vp_h = at("vp_h", [P, 2, 4, P], F32R, o_vp)
        vp_l = at("vp_l", [P, 2, 4, P], F32R, o_vp + 4096)
        pb, o_pb = sb("pb", [P, 4, HALF])
        xn2 = at("xn2", [P, 2, D], F32, o_pb)
        sg = at("sg", [P, 2, HALF], F32, o_pb)
        hf = at("hf", [P, 2, HALF], F32, o_pb + 4096)
        wo_raw = at("wo_raw", [P, 2, D], F32, o_pb)
        kn, _ = sb("kn", [P, 2, 2 * P])
        ident, _ = sb("ident", [P, P])
        nmx, _ = sb("nmx", [P, 4, 4])
        sums, _ = sb("sums", [P, 4, 4])
        rinv, _ = sb("rinv", [P, 4, 4])
        st, _ = sb("st", [P, 2, 12])
        mv, _ = sb("mv", [P, NB, 2])
        ve, _ = sb("ve", [P, NB])
        rstd, _ = sb("rstd", [P, NB])
        mhalf, _ = sb("mhalf", [P, 1])
        gates, _ = sb("gates", [P, 2])
        tg, _ = sb("tg", [P, 2])

        ps = ctx.enter_context(nc.psum_tensor("ps", [P, 8, HALF], F32))

        def sem(name):
            return ctx.enter_context(nc.semaphore(name))

        ident_zero = sem("ident_zero")
        consts = sem("consts")
        gates_in = sem("gates_in")
        wc_in = [sem("wc_in0"), sem("wc_in1")]
        wr_in = sem("wr_in")
        wo_in = [sem("wo_in0"), sem("wo_in1")]
        kv_in = [[sem(f"kv_in{i}_{h}") for h in range(2)] for i in range(NKV)]
        ct_first = sem("ct_first")
        ct_in = [sem("ct_in0"), sem("ct_in1")]
        x1_in = sem("x1_in")
        xn_in = sem("xn_in")
        stored = sem("stored")
        wc_hi, wc_lo = sem("wc_hi"), sem("wc_lo")
        wr_hi, wr_lo = sem("wr_hi"), sem("wr_lo")
        ct_hi, ct_lo = sem("ct_hi"), sem("ct_lo")
        first_hi, first_lo = sem("first_hi"), sem("first_lo")
        q_hi, q_lo = sem("q_hi"), sem("q_lo")
        pt_hi, pt_lo = sem("pt_hi"), sem("pt_lo")
        o_hi, o_lo = sem("o_hi"), sem("o_lo")
        v_hi, v_lo = sem("v_hi"), sem("v_lo")
        k_hi, k_lo = sem("k_hi"), sem("k_lo")
        xt1_hi, xt1_lo = sem("xt1_hi"), sem("xt1_lo")
        xt2_hi, xt2_lo = sem("xt2_hi"), sem("xt2_lo")
        h_hi, h_lo = sem("h_hi"), sem("h_lo")
        wc_used = sem("wc_used")
        o_first = sem("o_first")
        o_done = sem("o_done")
        s_done = sem("s_done")
        pt_done = sem("pt_done")
        pv_done = sem("pv_done")
        kv_done = sem("kv_done")
        kt_done = sem("kt_done")
        xt1_done, xt2_done = sem("xt1_done"), sem("xt2_done")
        y_done = sem("y_done")
        passed = sem("passed")
        tg_ready = sem("tg_ready")
        kb_zero = sem("kb_zero")
        kb_built = sem("kb_built")
        vp_built = sem("vp_built")
        maxed = sem("maxed")
        exped = sem("exped")
        inverted = sem("inverted")
        normed = sem("normed")
        k_nat = sem("k_nat")
        x1_add = sem("x1_add")
        st1, st2 = sem("st1"), sem("st2")
        mv1, mv2 = sem("mv1"), sem("mv2")
        ve_ready = sem("ve_ready")
        rs1, rs2 = sem("rs1"), sem("rs2")
        xn1_ready, xn2_ready = sem("xn1_ready"), sem("xn2_ready")
        gate_free = sem("gate_free")
        up_free = sem("up_free")
        y_free = sem("y_free")

        def column_slot(i):
            e = extra_slot(i)
            if e is None:
                return wc_h[:, i % CS, :, :], wc_l[:, i % CS, :, :]
            return wx_h[:, e, :, :], wx_l[:, e, :, :]

        def wcn(g, i, last):
            return g * NC + (NKV + i - (NKV if last and i >= WFF else 0))

        def used(g, i):
            return g * (NC - NKV) + (i + 1 - (NKV if i >= WFF else 0))

        def wc_arrived(g, i, last):
            per = (NC + 1) // 2 if i % 2 == 0 else NC // 2
            before = i // 2 - (NKV // 2 if last and i >= WFF else 0)
            return g * (16 * per) + 16 * (before + 1)

        def ct_arrived(G, b):
            return G * 32 + 16 * (b // 2 + 1)

        block = ctx.enter_context(nc.Block())

        @block.sync
        def _(sp):
            def load_wc(g, i, last, src=None):
                sp.wait_ge(wc_lo, wcn(g, i, last) - (0 if i == 0 else 1))
                sp.dma_start(wc_raw[:, i % 2, :], wc[i] if src is None else src).then_inc(wc_in[i % 2], 16)

            def load_wr(g, i, src=None):
                if i > 0:
                    sp.wait_ge(wr_lo, g * NR + (i if i != 7 else 5))
                sp.dma_start(wr_raw[:, :], wr[i] if src is None else src).then_inc(wr_in, 16)

            def load_ct(G, b, src):
                if b >= 2:
                    sp.wait_ge(ct_lo, G * NB + (b - 1))
                sp.dma_start(ct_raw[:, b % 2, :], src).then_inc(ct_in[b % 2], 16)

            def body(g, last):
                load_wc(g, 4, last)
                load_wr(g, 0)
                load_wc(g, 5, last)
                load_wc(g, 6, last)
                load_wr(g, 1)
                load_wc(g, 7, last)
                for i in (12, 13) if last else (8, 9):
                    load_wc(g, i, last)
                for i in (2, 3, 4):
                    load_wr(g, i)
                sp.wait_ge(pt_done, g * UNITS + UNITS)
                for i in (5, 6):
                    sp.dma_start(wo_raw[:, i - 5, :], wr[i]).then_inc(wo_in[i - 5], 16)
                if not last:
                    load_wc(g, 10, last)
                    load_wc(g, 11, last)
                sp.wait_ge(pv_done, g * PAIRS + PAIRS)
                if not last:
                    for b in range(2):
                        load_ct(g + 1, b, ctx_t[bass.ds(g * NB + (NB + b), 1), :, :].rearrange("o p n -> (o p) n"))
                load_wr(g, 7)
                src = x[g * NB:(g + 1) * NB] if last else x[bass.ds(g * NB, NB), :, :]
                sp.dma_start(x1[:, :, :], src.rearrange("t p n -> p t n")).then_inc(x1_in, 16)
                if not last:
                    load_wc(g, 12, last)
                    load_wc(g, 13, last)
                    for b in range(2, NB):
                        load_ct(g + 1, b, ctx_t[bass.ds(g * NB + (NB + b), 1), :, :].rearrange("o p n -> (o p) n"))
                load_wr(g, 8)
                load_wc(g, 14, last)
                load_wc(g, 15, last)
                if not last:
                    sp.wait_ge(kv_done, g * NB + 2 * NB)
                    src = x[bass.ds(g * NB + NB, NB), :, :]
                    sp.dma_start(xn[:, :, :], src.rearrange("t p n -> p t n")).then_inc(xn_in, 16)
                with sp.Fori(0, LOOPS) as i:
                    for c in range(4):
                        for n in (16 + 2 * c, 17 + 2 * c):
                            sp.wait_ge(wc_lo, wcn(g, n, last) - 1 + i * 8)
                            sp.dma_start(wc_raw[:, n % 2, :],
                                         wc[bass.ds(i * 8 + n, 1), :, :].rearrange("o p n -> (o p) n")
                                         ).then_inc(wc_in[n % 2], 16)
                        n = 9 + c
                        sp.wait_ge(wr_lo, g * NR + n + i * 4)
                        sp.dma_start(wr_raw[:, :],
                                     wr[bass.ds(i * 4 + n, 1), :, :].rearrange("o p n -> (o p) n")
                                     ).then_inc(wr_in, 16)
                for f in range(4 * LOOPS, FT):
                    for n in (16 + 2 * f, 17 + 2 * f):
                        if n < NC:
                            load_wc(g, n, last)
                        elif n > NC and not last:
                            load_wc(g + 1, n - NC - 1, False)
                    if 9 + f < NR:
                        load_wr(g, 9 + f)
                for t in range(NB):
                    sp.wait_ge(y_free, g * (CHUNKS * YN) + (4 + (CHUNKS - 1) * YN + 2 * t + 2))
                    dst = out[g * NB + t] if last else out[bass.ds(g * NB + t, 1), :, :].rearrange("o p n -> (o p) n")
                    sp.dma_start(dst, x1[:, t, :]).then_inc(stored, 16)

            sp.sem_inc(stored, 1)
            for h in range(2):
                cols = slice(h * HALF, (h + 1) * HALF)
                sp.dma_start(ct_raw[:, 0, cols], ctx_t[0, :, cols]).then_inc(ct_in[0] if h else ct_first, 16)
                for i in range(NKV):
                    sp.dma_start(kv_raw[:, i, cols], wc[WKV + i, :, cols]).then_inc(kv_in[i][h], 16)
            sp.dma_start(gates[:, 0:1], bass.AP(g_xattn.tensor, 0, [[0, P], [1, 1]])).then_inc(gates_in, 16)
            sp.dma_start(gates[:, 1:2], bass.AP(g_ffn.tensor, 0, [[0, P], [1, 1]])).then_inc(gates_in, 16)
            load_ct(0, 1, ctx_t[1])
            sp.dma_start(x1[:, :, :], x[0:NB].rearrange("t p n -> p t n")).then_inc(xn_in, 16)
            load_ct(0, 2, ctx_t[2])
            for i in range(2):
                sp.dma_start(wc_raw[:, i, :], wc[i]).then_inc(wc_in[i], 16)
            load_ct(0, 3, ctx_t[3])
            for i in (2, 3):
                load_wc(0, i, False)
            with sp.Fori(0, NG - 1) as g:
                body(g, False)
            body(NG - 1, True)
            sp.wait_ge(stored, 16 * NB * NG + 1)

        @block.gpsimd
        def _(pool):
            nc.gpsimd.memset(mhalf[:, :], -0.5)
            nc.gpsimd.memset(ident[:, :], 0.0).then_inc(ident_zero, 1)
            pool.wait_ge(ident_zero, 1)
            nc.gpsimd.affine_select(out=ident[:, :], in_=ident[:, :], compare_op=ALU.not_equal, fill=1.0,
                                    base=0, pattern=[[-1, P]], channel_multiplier=1).then_inc(consts, 1)
            pool.wait_ge(consts, 1)

            def rsqrt(G, t, mv_ready, calls, done):
                pool.wait_ge(mv_ready, G * NB + (t + 1))
                pool.sem_inc(passed, 1)
                nc.gpsimd.tensor_scalar(ve[:, t:t + 1], mv[:, t, 1:2], EPS, None, ALU.add).then_inc(ve_ready, 1)
                pool.wait_ge(ve_ready, calls)
                nc.gpsimd.tensor_tensor(rstd[:, t:t + 1], ve[:, t:t + 1], mhalf[:, :], ALU.pow).then_inc(done, 1)

            def body(g, last):
                pool.wait_ge(xt1_done, g * 8 + 8)
                pool.wait_ge(kv_done, g * NB + NB)
                pool.sem_inc(passed, 1)
                for buf in (kb_h, kb_l, vp_h, vp_l):
                    ins = nc.gpsimd.memset(buf[:, :, :].bitcast(F32) if buf in (kb_h, kb_l)
                                           else buf[:, :, :, :].bitcast(F32), 0.0)
                ins.then_inc(kb_zero, 1)
                for n in range(UNITS):
                    pool.wait_ge(inverted, g * UNITS + (n + 1))
                    p = pb[:, n % 4, :].rearrange("p (j k) -> p j k", j=4)
                    r = bass.AP(rinv, (n % 4) * 4, [[16, P], [1, 4], [0, P]])
                    nc.gpsimd.tensor_tensor(p, p, r, ALU.mult).then_inc(normed, 1)
                for t in range(NB):
                    rsqrt(g, t, mv2, g * (2 * NB) + (NB + t + 1), rs2)
                if not last:
                    for t in range(NB):
                        rsqrt(g + 1, t, mv1, g * (2 * NB) + (2 * NB + t + 1), rs1)

            for t in range(NB):
                rsqrt(0, t, mv1, t + 1, rs1)
            with pool.Fori(0, NG - 1) as g:
                body(g, False)
            body(NG - 1, True)

        @block.scalar
        def _(act):
            def copy(out, in_, scale=1.0):
                return nc.scalar.activation(out, in_, ACT.Copy, scale=scale)

            def split_wc(g, i, last, extra=0):
                act.wait_ge(wc_in[i % 2], wc_arrived(g, i, last) + extra)
                copy(column_slot(i)[0], wc_raw[:, i % 2, :].rearrange("p (k m) -> p k m", k=K8)).then_inc(wc_hi, 1)

            def split_wr(g, i, extra=0):
                if i in (5, 6):
                    act.wait_ge(wo_in[i - 5], g * 16 + 16)
                    copy(wr_h[:, i % RS, :], wo_raw[:, i - 5, :]).then_inc(wr_hi, 1)
                else:
                    act.wait_ge(wr_in, g * (16 * (NR - 2)) + 16 * (i + 1 if i < 5 else i - 1) + extra)
                    copy(wr_h[:, i % RS, :], wr_raw[:, :]).then_inc(wr_hi, 1)

            def split_ct(G, b):
                act.wait_ge(ct_in[b % 2], ct_arrived(G, b))
                if b >= 2:
                    act.wait_ge(kv_done, G * NB + (b - 1))
                copy(ct_h[:, b % 2, :, :], ct_raw[:, b % 2, :].rearrange("p (k m) -> p k m", k=K8)).then_inc(ct_hi, 1)

            def kv_out(G, b):
                act.wait_ge(kv_done, G * NB + (b + 1))
                if b >= 2:
                    act.wait_ge(kt_done, G * NB + (b - 1))
                copy(kn[:, b % 2, :], ps[:, b % 2, 0:2 * P]).then_inc(k_nat, 1)
                copy(vc_h[:, b, :], ps[:, b % 2, 2 * P:4 * P]).then_inc(v_hi, 1)

            def kt_out(G, b):
                act.wait_ge(kt_done, G * NB + (b + 1))
                copy(kc_h[:, :, b * P:(b + 1) * P],
                     ps[:, 2 + b % 2, 0:2 * P].rearrange("p (a m) -> p a m", a=2)).then_inc(k_hi, 1)

            def xt_out(G, t, h, done, hi, bank):
                act.wait_ge(done, G * 8 + (2 * t + h + 1))
                copy(xt_h[:, 4 * h:4 * h + 4, t * P:(t + 1) * P],
                     ps[:, bank, :].rearrange("p (k m) -> p k m", k=4)).then_inc(hi, 1)

            def q_out(g, i):
                act.wait_ge(wc_used, used(g, i))
                copy(qo_h[0:H2, i, :], ps[0:H2, q_bank(i), :], SCALE)
                copy(qo_l[H2:P, i, :], ps[H2:P, q_bank(i), :], SCALE).then_inc(q_hi, 1)

            def pt_out(g, n):
                m, gi = n // 2, n % 2
                act.wait_ge(pt_done, g * UNITS + (n + 1))
                if m >= 2:
                    act.wait_ge(pv_done, g * PAIRS + (m - 1))
                copy(pt_h[:, m % 2, :, gi * P:(gi + 1) * P],
                     ps[:, 3 + n % 2, :].rearrange("p (j q) -> p j q", j=4)).then_inc(pt_hi, 1)

            def exps(g, n):
                act.wait_ge(maxed, g * UNITS + (n + 1))
                if n >= 4:
                    act.wait_ge(pt_done, g * UNITS + (n - 3))
                for j in range(4):
                    ins = nc.scalar.activation(pb[:, n % 4, j * P:(j + 1) * P], ps[:, n % 3, j * P:(j + 1) * P],
                                               ACT.Exp, bias=nmx[:, n % 4, j:j + 1],
                                               accum_out=sums[:, n % 4, j:j + 1])
                ins.then_inc(exped, 1)

            def o_out(g, m):
                k, b = m // NB, m % NB
                act.wait_ge(pv_done, g * PAIRS + (m + 1))
                copy(qo_h[:, 2 * k:2 * k + 2, b * P:(b + 1) * P],
                     ps[:, 5, 0:2 * P].rearrange("p (g q) -> p g q", g=2)).then_inc(o_hi, 1)

            def hidden(g, f, fi, before, after):
                s = f % 2
                rows = P if f != MIX else FR
                act.wait_ge(wc_used, used(g, gate_tile(f)) + fi * 8)
                act.wait_ge(up_free, g * FT + (f + (1 if f < MIX else 2)) + fi * 4)
                if f == MIX:
                    nc.scalar.activation(sg[0:FR, 0, :], ps[0:FR, 0, :], ACT.Silu)
                    copy(sg[0:FR, 1, :], ps[FR:P, 0, :]).then_inc(gate_free, 1)
                else:
                    nc.scalar.activation(sg[:, s, :], ps[:, 2 * s, :], ACT.Silu).then_inc(gate_free, 1)
                before()
                act.wait_ge(up_free, g * FT + (f + 3) + fi * 4)
                copy(h_h[0:rows, f % 4, :], hf[0:rows, s, :]).then_inc(h_hi, 1)
                after()

            def body(g, last):
                split_wc(g, 4, last)
                q_out(g, 0)
                q_out(g, 1)
                act.wait_ge(stored, g * (16 * NB) + 1)
                for n in range(STEPS + 1):
                    if n >= 7 and n % 2 == 1:
                        o_out(g, (n - 7) // 2)
                    if 3 <= n < UNITS + 3:
                        pt_out(g, n - 3)
                    if n < UNITS:
                        exps(g, n)
                    if n % 4 == 2 and n < UNITS - 8:
                        q_out(g, n // 4 + 2)
                    for i in COL_STEP:
                        if COL_STEP[i] == n and not (last and i >= WKV):
                            split_wc(g, i, last)
                    for i in ROW_STEP:
                        if ROW_STEP[i] == n:
                            split_wr(g, i)
                for e in range(4):
                    act.wait_ge(o_first, g * 4 + (e + 1))
                    split_wr(g, 4 + e)
                if not last:
                    split_wc(g, WKV + 2, last)
                    split_wc(g, WKV + 3, last)
                    split_ct(g + 1, 0)
                    split_ct(g + 1, 1)
                G = g + 1

                def xt2(t):
                    for h in range(2):
                        xt_out(g, t, h, xt2_done, xt2_hi, 4 + 2 * (t % 2) + h)
                if last:
                    act.wait_ge(o_done, g * NB + NB)
                    split_wc(g, WFF, last)
                    xt2(0)
                    xt2(1)
                    split_wc(g, WFF + 1, last)
                    xt2(2)
                    xt2(3)
                    split_wc(g, WFF + 2, last)
                    split_wc(g, WFF + 3, last)
                else:
                    kv_out(G, 0)
                    split_ct(G, 2)
                    kv_out(G, 1)
                    split_ct(G, 3)
                    kt_out(G, 0)
                    xt2(0)
                    xt2(1)
                    kv_out(G, 2)
                    kt_out(G, 1)
                    split_wc(g, WFF, last)
                    xt2(2)
                    xt2(3)
                    split_wc(g, WFF + 1, last)
                    kv_out(G, 3)
                    kt_out(G, 2)
                    kt_out(G, 3)
                    split_wc(g, WFF + 2, last)
                    split_wc(g, WFF + 3, last)
                with act.Fori(0, LOOPS) as i:
                    for c in range(4):
                        def before(c=c):
                            split_wr(g, 8 + c, i * 64)
                            split_wc(g, 16 + 2 * c, last, i * 64)

                        def after(c=c):
                            split_wc(g, 17 + 2 * c, last, i * 64)
                        hidden(g, c, i, before, after)
                for f in range(4 * LOOPS, FT):
                    def before(f=f):
                        if f < MIX:
                            split_wr(g, 8 + f)
                            split_wc(g, 16 + 2 * f, last)
                        else:
                            if not last:
                                split_wc(G, f - MIX, False)
                            split_wr(g, 8 + f)

                    def after(f=f):
                        if 17 + 2 * f < NC:
                            split_wc(g, 17 + 2 * f, last)
                    hidden(g, f, 0, before, after)
                if not last:
                    for q in range(2 * NB):
                        xt_out(G, q // 2, q % 2, xt1_done, xt1_hi, TR_BANKS[q % 4])
                        if q in (3, 5):
                            split_wc(G, 2 + q // 5, False)

            for h in range(2):
                ks, cols = slice(4 * h, 4 * h + 4), slice(h * HALF, (h + 1) * HALF)
                act.wait_ge(ct_in[0] if h else ct_first, 16)
                copy(ct_h[:, 0, ks, :], ct_raw[:, 0, cols].rearrange("p (k m) -> p k m", k=4)
                     ).then_inc(ct_hi if h else first_hi, 1)
                for i in range(NKV):
                    act.wait_ge(kv_in[i][h], 16)
                    copy(wc_h[:, i, ks, :], kv_raw[:, i, cols].rearrange("p (k m) -> p k m", k=4)
                         ).then_inc(wc_hi if h else first_hi, 1)
            split_ct(0, 1)
            act.wait_ge(gates_in, 32)
            nc.scalar.activation(tg[:, :], gates[:, :], ACT.Tanh).then_inc(tg_ready, 1)
            act.wait_ge(tg_ready, 1)
            copy(tg[:, :], tg[:, :]).then_inc(gate_free, 2)

            def xt1(t):
                for h in range(2):
                    xt_out(0, t, h, xt1_done, xt1_hi, 4 + 2 * (t % 2) + h)
            kv_out(0, 0)
            split_ct(0, 2)
            kv_out(0, 1)
            split_ct(0, 3)
            kt_out(0, 0)
            xt1(0)
            kv_out(0, 2)
            kt_out(0, 1)
            xt1(1)
            split_wc(0, 0, False)
            xt1(2)
            xt1(3)
            split_wc(0, 1, False)
            kv_out(0, 3)
            kt_out(0, 2)
            kt_out(0, 3)
            split_wc(0, 2, False)
            split_wc(0, 3, False)
            with act.Fori(0, NG - 1) as g:
                body(g, False)
            body(NG - 1, True)

        @block.vector
        def _(dve):
            def minus(out, whole, hi):
                return nc.vector.tensor_tensor(out, whole, hi.bitcast(F32), ALU.subtract)

            def split_wc(g, i, last, extra=0):
                dve.wait_ge(wc_hi, wcn(g, i, last) + 1 + extra)
                hi, lo = column_slot(i)
                minus(lo, wc_raw[:, i % 2, :].rearrange("p (k m) -> p k m", k=K8), hi).then_inc(wc_lo, 1)

            def split_wr(g, i, extra=0):
                dve.wait_ge(wr_hi, g * NR + (i + 1) + extra)
                raw = wo_raw[:, i - 5, :] if i in (5, 6) else wr_raw[:, :]
                minus(wr_l[:, i % RS, :], raw, wr_h[:, i % RS, :]).then_inc(wr_lo, 1)

            def split_ct(G, b):
                dve.wait_ge(ct_hi, G * NB + (b + 1))
                minus(ct_l[:, b % 2, :, :], ct_raw[:, b % 2, :].rearrange("p (k m) -> p k m", k=K8),
                      ct_h[:, b % 2, :, :]).then_inc(ct_lo, 1)

            def v_out(G, b):
                dve.wait_ge(v_hi, G * NB + (b + 1))
                minus(vc_l[:, b, :], ps[:, b % 2, 2 * P:4 * P], vc_h[:, b, :]).then_inc(v_lo, 1)

            def k_out(G, b):
                dve.wait_ge(k_hi, G * NB + (b + 1))
                minus(kc_l[:, :, b * P:(b + 1) * P], ps[:, 2 + b % 2, 0:2 * P].rearrange("p (a m) -> p a m", a=2),
                      kc_h[:, :, b * P:(b + 1) * P]).then_inc(k_lo, 1)

            def xt_out(G, t, h, hi, lo, bank):
                dve.wait_ge(hi, G * 8 + (2 * t + h + 1))
                where = (slice(None), slice(4 * h, 4 * h + 4), slice(t * P, (t + 1) * P))
                minus(xt_l[where], ps[:, bank, :].rearrange("p (k m) -> p k m", k=4), xt_h[where]).then_inc(lo, 1)

            def q_out(g, i):
                dve.wait_ge(q_hi, g * NQ + (i + 1))
                for q, rows, others in ((qo_h, slice(0, H2), slice(H2, P)), (qo_l, slice(H2, P), slice(0, H2))):
                    ins = nc.vector.scalar_tensor_tensor(q[others, i, :], ps[rows, q_bank(i), :], SCALE,
                                                         q[rows, i, :].bitcast(F32), ALU.mult, ALU.subtract)
                ins.then_inc(q_lo, 1)

            def build_kb(g, a, b):
                for j in range(4):
                    for half in range(2):
                        rows = slice(half * H2 + j % 2 * HD, half * H2 + j % 2 * HD + HD)
                        src = slice(j * HD, (j + 1) * HD)
                        keys, cols = slice(b * P, (b + 1) * P), slice(j * P, (j + 1) * P)
                        nc.vector.tensor_copy(kb_h[rows, b, cols], kc_h[src, a, keys].bitcast(F32))
                        if rows == src:
                            ins = nc.vector.tensor_copy(kb_l[rows, b, cols], kc_l[src, a, keys].bitcast(F32))
                ins.then_inc(kb_built, 1)

            def build_vp(g, m):
                a, b = m // NB // 2, m % NB
                for vp, vc in ((vp_h, vc_h), (vp_l, vc_l)):
                    dst = bass.AP(vp, (m % 2) * 4 * P, [[8 * P, P], [P + HD, 4], [1, HD]])
                    ins = nc.vector.tensor_copy(dst, vc[:, b, a * P:(a + 1) * P].rearrange("p (j d) -> p j d", j=4).bitcast(F32))
                ins.then_inc(vp_built, 1)

            def row_max(g, n):
                dve.wait_ge(s_done, g * UNITS + (n + 1))
                nc.vector.tensor_reduce(nmx[:, n % 4, :], ps[:, n % 3, :].rearrange("p (j k) -> p j k", j=4),
                                        AX_X, ALU.max, negate=True).then_inc(maxed, 1)

            def invert(g, n):
                dve.wait_ge(exped, g * UNITS + (n + 1))
                nc.vector.reciprocal(rinv[:, n % 4, :], sums[:, n % 4, :]).then_inc(inverted, 1)

            def pt_out(g, n):
                m, gi = n // 2, n % 2
                dve.wait_ge(pt_hi, g * UNITS + (n + 1))
                where = (slice(None), m % 2, slice(None), slice(gi * P, (gi + 1) * P))
                minus(pt_l[where], ps[:, 3 + n % 2, :].rearrange("p (j q) -> p j q", j=4), pt_h[where]).then_inc(pt_lo, 1)

            def o_out(g, m):
                k, b = m // NB, m % NB
                dve.wait_ge(o_hi, g * PAIRS + (m + 1))
                where = (slice(None), slice(2 * k, 2 * k + 2), slice(b * P, (b + 1) * P))
                minus(qo_l[where], ps[:, 5, 0:2 * P].rearrange("p (g q) -> p g q", g=2), qo_h[where]).then_inc(o_lo, 1)

            def stats(G, t, src, counted, done):
                for h in range(2):
                    ins = nc.vector.bn_stats(st[:, t % 2, 6 * h:6 * h + 6], src[:, t, h * HALF:(h + 1) * HALF])
                ins.then_inc(counted, 1)
                dve.wait_ge(counted, G * NB + (t + 1))
                dve.sem_inc(passed, 1)
                nc.vector.bn_aggr(mv[:, t, :], st[:, t % 2, :]).then_inc(done, 1)

            def normalise(G, t, dst, src, rs, done):
                dve.wait_ge(rs, G * NB + (t + 1))
                nc.vector.tensor_scalar(dst, src, mv[:, t, 0:1], rstd[:, t:t + 1],
                                        ALU.subtract, ALU.mult).then_inc(done, 1)

            def hidden(g, f, fi, before, after):
                s = f % 2
                rows = P if f != MIX else FR
                dve.wait_ge(gate_free, g * FT + (f + 3) + fi * 4)
                if f == MIX:
                    nc.vector.tensor_tensor(hf[0:FR, s, :], sg[0:FR, 0, :], sg[0:FR, 1, :], ALU.mult).then_inc(up_free, 1)
                    before()
                else:
                    before()
                    dve.wait_ge(wc_used, used(g, gate_tile(f) + 1) + fi * 8)
                    nc.vector.tensor_tensor(hf[:, s, :], sg[:, s, :], ps[:, 2 * s + 1, :], ALU.mult).then_inc(up_free, 1)
                dve.wait_ge(h_hi, g * FT + (f + 1) + fi * 4)
                lo = h_l[:, f % 4, :] if f != MIX else h_h[FR:2 * FR, f % 4, :]
                minus(lo, hf[0:rows, s, :], h_h[0:rows, f % 4, :]).then_inc(h_lo, 1)
                after()

            def add_y(g, c, fi, ids=range(YN)):
                for idx in ids:
                    t, d = idx // NH, idx % NH
                    dve.wait_ge(y_done, g * (CHUNKS * YN) + (c * YN + idx + 1) + fi * (2 * YN))
                    place = x1[:, t, d * HALF:(d + 1) * HALF]
                    nc.vector.scalar_tensor_tensor(place, ps[:, 4 + idx % 4, :], tg[:, 1:2], place,
                                                   ALU.mult, ALU.add).then_inc(y_free, 1)

            def body(g, last):
                dve.wait_ge(kb_zero, g + 1)
                dve.wait_ge(k_lo, g * NB + NB)
                dve.wait_ge(v_lo, g * NB + NB)
                for b in range(NB):
                    build_kb(g, 0, b)
                build_vp(g, 0)
                build_vp(g, 1)
                split_wc(g, 4, last)
                q_out(g, 0)
                q_out(g, 1)
                for n in range(STEPS + 1):
                    if n < UNITS:
                        row_max(g, n)
                    if 1 <= n < UNITS + 1:
                        invert(g, n - 1)
                    if n % 4 == 3 and n < UNITS - 8:
                        q_out(g, n // 4 + 2)
                    for i in COL_STEP:
                        if COL_STEP[i] + 1 == n and not (last and i >= WKV):
                            split_wc(g, i, last)
                    for i in ROW_STEP:
                        if ROW_STEP[i] + 1 == n:
                            split_wr(g, i)
                    if n >= 7 and n % 2 == 1:
                        m = (n - 7) // 2
                        o_out(g, m)
                        if m + 2 < PAIRS:
                            build_vp(g, m + 2)
                    if 3 <= n < UNITS + 3:
                        pt_out(g, n - 3)
                    if n in KB_STEPS:
                        b = KB_STEPS.index(n)
                        dve.wait_ge(s_done, g * UNITS + (8 + 2 * b + 2))
                        build_kb(g, 1, b)
                for e in range(4):
                    split_wr(g, 4 + e)
                if not last:
                    split_wc(g, WKV + 2, last)
                    split_wc(g, WKV + 3, last)
                    split_ct(g + 1, 0)
                    split_ct(g + 1, 1)
                G = g + 1
                dve.wait_ge(x1_in, g * 16 + 16)
                for t in range(NB):
                    dve.wait_ge(o_done, g * NB + (t + 1))
                    for d in range(NH):
                        place = x1[:, t, d * HALF:(d + 1) * HALF]
                        nc.vector.scalar_tensor_tensor(place, ps[:, 2 * t + d, :], tg[:, 0:1], place,
                                                       ALU.mult, ALU.add).then_inc(x1_add, 1)
                    dve.wait_ge(x1_add, g * YN + (2 * t + 2))
                    stats(g, t, x1, st2, mv2)
                    if t < 2:
                        normalise(g, t, xn2[:, t % 2, :], x1[:, t, :], rs2, xn2_ready)

                def xt2(t):
                    for h in range(2):
                        xt_out(g, t, h, xt2_hi, xt2_lo, 4 + 2 * (t % 2) + h)
                    if t < 2:
                        normalise(g, t + 2, xn2[:, t % 2, :], x1[:, t + 2, :], rs2, xn2_ready)
                if last:
                    split_wc(g, WFF, last)
                    xt2(0)
                    xt2(1)
                    split_wc(g, WFF + 1, last)
                    xt2(2)
                    xt2(3)
                    split_wc(g, WFF + 2, last)
                    split_wc(g, WFF + 3, last)
                else:
                    v_out(G, 0)
                    split_ct(G, 2)
                    v_out(G, 1)
                    split_ct(G, 3)
                    k_out(G, 0)
                    xt2(0)
                    xt2(1)
                    v_out(G, 2)
                    k_out(G, 1)
                    split_wc(g, WFF, last)
                    xt2(2)
                    xt2(3)
                    split_wc(g, WFF + 1, last)
                    v_out(G, 3)
                    k_out(G, 2)
                    k_out(G, 3)
                    split_wc(g, WFF + 2, last)
                    split_wc(g, WFF + 3, last)
                with dve.Fori(0, LOOPS) as i:
                    for c in range(4):
                        def before(c=c):
                            split_wr(g, 8 + c, i * 4)
                            split_wc(g, 16 + 2 * c, last, i * 8)

                        def after(c=c):
                            split_wc(g, 17 + 2 * c, last, i * 8)
                        hidden(g, c, i, before, after)
                    add_y(g, 0, i)
                    add_y(g, 1, i)
                for f in range(4 * LOOPS, FT):
                    t = f - 4 * LOOPS
                    if t < NB and not last:
                        if t == 0:
                            dve.wait_ge(xn_in, g * 16 + 32)
                        stats(G, t, xn, st1, mv1)

                    def before(f=f):
                        if f < MIX:
                            split_wr(g, 8 + f)
                            split_wc(g, 16 + 2 * f, last)
                        else:
                            if not last:
                                split_wc(G, f - MIX, False)
                            split_wr(g, 8 + f)

                    def after(f=f):
                        if 17 + 2 * f < NC:
                            split_wc(g, 17 + 2 * f, last)
                    hidden(g, f, 0, before, after)
                    if t < NB and not last:
                        normalise(G, t, xn[:, t, :], xn[:, t, :], rs1, xn1_ready)
                    if t == 3:
                        add_y(g, 8, 0)
                        add_y(g, 9, 0)
                if last:
                    add_y(g, 10, 0)
                else:
                    def xt1(t):
                        for h in range(2):
                            xt_out(G, t, h, xt1_hi, xt1_lo, TR_BANKS[(2 * t + h) % 4])
                    xt1(0)
                    xt1(1)
                    add_y(g, 10, 0, (0, 1))
                    split_wc(G, 2, False)
                    xt1(2)
                    add_y(g, 10, 0, (2, 3))
                    xt1(3)
                    split_wc(G, 3, False)
                    add_y(g, 10, 0, (4, 5, 6, 7))

            nc.vector.memset(st[:, 0, :], 0.0).then_inc(up_free, 2)
            nc.vector.memset(st[:, 1, :], 0.0).then_inc(y_free, 4)
            dve.wait_ge(up_free, 2)
            dve.wait_ge(y_free, 4)
            for h in range(2):
                ks, cols = slice(4 * h, 4 * h + 4), slice(h * HALF, (h + 1) * HALF)
                dve.wait_ge(ct_hi if h else first_hi, 1)
                minus(ct_l[:, 0, ks, :], ct_raw[:, 0, cols].rearrange("p (k m) -> p k m", k=4),
                      ct_h[:, 0, ks, :]).then_inc(ct_lo if h else first_lo, 1)
                for i in range(NKV):
                    dve.wait_ge(wc_hi if h else first_hi, i + (1 if h else 2))
                    minus(wc_l[:, i, ks, :], kv_raw[:, i, cols].rearrange("p (k m) -> p k m", k=4),
                          wc_h[:, i, ks, :]).then_inc(wc_lo if h else first_lo, 1)
            split_ct(0, 1)
            dve.wait_ge(gate_free, 2)
            dve.wait_ge(xn_in, 16)
            def normalise_first(t):
                normalise(0, t, x1[:, t, :], x1[:, t, :], rs1, xn1_ready)
            stats(0, 0, x1, st1, mv1)
            stats(0, 1, x1, st1, mv1)
            normalise_first(0)
            v_out(0, 0)
            split_ct(0, 2)
            stats(0, 2, x1, st1, mv1)
            normalise_first(1)
            v_out(0, 1)
            split_ct(0, 3)
            stats(0, 3, x1, st1, mv1)
            normalise_first(2)

            def xt1(t):
                for h in range(2):
                    xt_out(0, t, h, xt1_hi, xt1_lo, 4 + 2 * (t % 2) + h)
            k_out(0, 0)
            xt1(0)
            normalise_first(3)
            v_out(0, 2)
            k_out(0, 1)
            xt1(1)
            split_wc(0, 0, False)
            xt1(2)
            xt1(3)
            split_wc(0, 1, False)
            v_out(0, 3)
            k_out(0, 2)
            k_out(0, 3)
            split_wc(0, 2, False)
            split_wc(0, 3, False)
            with dve.Fori(0, NG - 1) as g:
                body(g, False)
            body(NG - 1, True)

        @block.tensor
        def _(pe):
            def three(out, w_h, w_l, m_h, m_l, first, last):
                pe.matmul(out, w_h, m_h, start=first, stop=False)
                pe.matmul(out, w_h, m_l, start=False, stop=False)
                return pe.matmul(out, w_l, m_h, start=False, stop=last)

            def column_tile(out, i, ks):
                hi, lo = column_slot(i)
                for k in ks:
                    ins = three(out, hi[:, k, :], lo[:, k, :], xt_h[:, k, :], xt_l[:, k, :],
                                k == 0, k == K8 - 1)
                return ins

            def q_tile(g, i, ks):
                if ks[0] == 0:
                    pe.wait_ge(wc_lo, wcn(g, i, False) + 1)
                    if i >= 4:
                        pe.wait_ge(q_lo, g * NQ + (i - 1))
                ins = column_tile(ps[:, q_bank(i), :], i, ks)
                if ks[-1] == K8 - 1:
                    ins.then_inc(wc_used, 1)

            def scores(g, n):
                k, b, gi = n // 8, n % 8 // 2, n % 2
                a, iq = k // 2, 2 * k + gi
                pe.wait_ge(q_lo, g * NQ + (iq + 1))
                pe.wait_ge(kb_built, g * (2 * NB) + (a * NB + b + 1))
                if n >= 3:
                    pe.wait_ge(exped, g * UNITS + (n - 2))
                toks = slice(b * P, (b + 1) * P)
                for q, cols in ((qo_h, slice(0, 2 * P)), (qo_l, slice(2 * P, 4 * P))):
                    pe.matmul(ps[:, n % 3, cols], q[:, iq, toks], kb_h[:, b, cols], start=True, stop=False)
                    ins = pe.matmul(ps[:, n % 3, cols], q[:, iq, toks], kb_l[:, b, cols], start=False, stop=True)
                ins.then_inc(s_done, 1)

            def transpose_p(g, n):
                pe.wait_ge(normed, g * UNITS + (n + 1))
                if n >= 2:
                    pe.wait_ge(pt_lo, g * UNITS + (n - 1))
                for j in range(4):
                    ins = pe.transpose(ps[:, 3 + n % 2, j * P:(j + 1) * P], pb[:, n % 4, j * P:(j + 1) * P], ident[:, :])
                ins.then_inc(pt_done, 1)

            def weigh_values(g, m):
                pe.wait_ge(pt_lo, g * UNITS + (2 * m + 2))
                pe.wait_ge(vp_built, g * PAIRS + (m + 1))
                if m >= 1:
                    pe.wait_ge(o_lo, g * PAIRS + m)
                for j in range(4):
                    ins = three(ps[:, 5, 0:2 * P], vp_h[:, m % 2, j, :], vp_l[:, m % 2, j, :],
                                pt_h[:, m % 2, j, :], pt_l[:, m % 2, j, :], j == 0, j == 3)
                ins.then_inc(pv_done, 1)

            def o_part(e, t, d):
                toks, cols = slice(t * P, (t + 1) * P), slice(d * HALF, (d + 1) * HALF)
                return three(ps[:, 2 * t + d, :], qo_h[:, e, toks], qo_l[:, e, toks],
                             wr_h[:, e % RS, cols], wr_l[:, e % RS, cols], e == 0, e == NO - 1)

            def kv(G, b, ks=range(K8)):
                if ks[-1] == K8 - 1:
                    pe.wait_ge(ct_lo, G * NB + (b + 1))
                if b >= 2:
                    pe.wait_ge(v_lo, G * NB + (b - 1))
                for k in ks:
                    ins = three(ps[:, b % 2, :].rearrange("p (s m) -> p s m", s=CS),
                                ct_h[:, b % 2, k, :], ct_l[:, b % 2, k, :], wc_h[:, :, k, :], wc_l[:, :, k, :],
                                k == 0, k == K8 - 1)
                if ks[-1] == K8 - 1:
                    ins.then_inc(kv_done, 1)

            def kt(G, b):
                pe.wait_ge(k_nat, G * NB + (b + 1))
                if b >= 2:
                    pe.wait_ge(k_lo, G * NB + (b - 1))
                for a in range(2):
                    ins = pe.transpose(ps[:, 2 + b % 2, a * P:(a + 1) * P], kn[:, b % 2, a * P:(a + 1) * P], ident[:, :])
                ins.then_inc(kt_done, 1)

            def xt(src, h, bank, done):
                for c in range(4):
                    k = 4 * h + c
                    ins = pe.transpose(ps[:, bank, c * P:(c + 1) * P], src[:, k * P:(k + 1) * P], ident[:, :])
                ins.then_inc(done, 1)

            def gate_up(g, f, fi, last):
                s = f % 2
                for u in range(2):
                    i = gate_tile(f) + u
                    pe.wait_ge(wc_lo, wcn(g, i, last) + 1 + fi * 8)
                    pe.wait_ge(up_free if u else gate_free, g * FT + (f + 1) + fi * 4)
                    if not last and f < 2 and f + u > 0:
                        pe.wait_ge(k_lo if f else v_lo, g * NB + (2 * NB - (1 if f and not u else 0)))
                    column_tile(ps[:, 2 * s + u, :], i, range(K8)).then_inc(wc_used, 1)

            def y_part(c, idx, us):
                t, d = idx // NH, idx % NH
                toks, cols = slice(t * P, (t + 1) * P), slice(d * HALF, (d + 1) * HALF)
                for u in us:
                    s, bank = (2 * c + u) % 4, ps[:, 4 + idx % 4, :]
                    if 2 * c + u == MIX:
                        pe.matmul(bank, h_h[:, s, toks], wr_h[:, s, cols], start=True, stop=False)
                        ins = pe.matmul(bank, h_h[0:FR, s, toks], wr_l[0:FR, s, cols], start=False, stop=False)
                    else:
                        ins = three(bank, h_h[:, s, toks], h_l[:, s, toks],
                                    wr_h[:, s, cols], wr_l[:, s, cols], u == 0, u == 1)
                return ins

            def down(g, c, fi, ids=range(YN)):
                if ids[0] == 0:
                    pe.wait_ge(wr_lo, g * NR + (NO + 2 * c + 2) + fi * 4)
                    pe.wait_ge(h_lo, g * FT + (2 * c + 2) + fi * 4)
                for idx in ids:
                    pe.wait_ge(y_free, g * (CHUNKS * YN) + (c * YN + idx + 1) + fi * (2 * YN))
                    y_part(c, idx, (0, 1)).then_inc(y_done, 1)

            def body(g, last):
                pe.wait_ge(xt1_lo, g * 8 + 8)
                pe.wait_ge(v_lo, g * NB + NB - 1)
                q_tile(g, 0, range(K8))
                pe.wait_ge(y_free, g * (CHUNKS * YN) + 4)
                q_tile(g, 1, range(K8))

                def q_part(w):
                    q_tile(g, 2 + w // 4, (w % 4 * 2, w % 4 * 2 + 1))
                q_part(0)
                q_part(1)
                for n in range(STEPS):
                    if n < UNITS - 10:
                        q_part(n + 2)
                    if n < UNITS:
                        scores(g, n)
                    if 3 <= n < UNITS + 3:
                        transpose_p(g, n - 3)
                    w = n - (UNITS - 10)
                    if 0 <= w < 4 * NH:
                        e, d = (w % 3, w // 3) if w < 6 else (3, w - 6)
                        if w == 0:
                            pe.wait_ge(o_lo, g * PAIRS + PAIRS // 2)
                        if e == 0:
                            pe.wait_ge(q_lo, g * NQ + (NQ - 1 + d))
                        if d == 0:
                            pe.wait_ge(wr_lo, g * NR + (e + 1))
                        o_part(e, NB - 1, d)
                    if n > UNITS:
                        if n == UNITS + 1:
                            pe.wait_ge(exped, g * UNITS + UNITS)
                        for w in (2 * (n - UNITS - 1), 2 * (n - UNITS - 1) + 1):
                            o_part(w // NH, 0, w % NH)
                    if n >= 6 and n % 2 == 0:
                        weigh_values(g, (n - 6) // 2)
                for e in range(4):
                    for d in range(NH):
                        o_part(e, 1, d)
                pe.wait_ge(o_lo, g * PAIRS + PAIRS)
                for e in range(4):
                    for d in range(NH):
                        ins = o_part(e, 2, d)
                    ins.then_inc(o_first, 1)
                for t in range(NB):
                    for e in range(4, NO):
                        if t == 0:
                            pe.wait_ge(wr_lo, g * NR + (e + 1))
                        for d in range(NH):
                            ins = o_part(e, t, d)
                    ins.then_inc(o_done, 1)
                G = g + 1

                def xt2(t):
                    pe.wait_ge(xn2_ready, g * NB + (t + 1))
                    for h in range(2):
                        if t < 2:
                            pe.wait_ge(x1_add, g * YN + (6 + 2 * t))
                        else:
                            pe.wait_ge(xt2_lo, g * 8 + (2 * (t - 2) + h + 1))
                        xt(xn2[:, t % 2, :], h, 4 + 2 * (t % 2) + h, xt2_done)
                if not last:
                    pe.wait_ge(wc_lo, wcn(g, WKV + 3, False) + 1)
                    pe.wait_ge(x1_add, g * YN + 2)
                    kv(G, 0)
                    kv(G, 1)
                    pe.wait_ge(x1_add, g * YN + 4)
                    kt(G, 0)
                    xt2(0)
                    xt2(1)
                    kv(G, 2)
                    kt(G, 1)
                    xt2(2)
                    xt2(3)
                    kv(G, 3)
                    kt(G, 2)
                    kt(G, 3)
                    pe.wait_ge(v_lo, g * NB + 2 * NB - 1)
                else:
                    for t in range(NB):
                        xt2(t)
                pe.wait_ge(xt2_lo, g * 8 + 8)
                pe.sem_inc(passed, 1)
                with pe.Fori(0, LOOPS) as i:
                    for c in range(4):
                        gate_up(g, c, i, last)
                    down(g, 0, i)
                    down(g, 1, i)
                for f in range(4 * LOOPS, 4 * LOOPS + 4):
                    gate_up(g, f, 0, last)
                down(g, 8, 0)
                down(g, 9, 0)
                pe.wait_ge(wc_lo, wcn(g, gate_tile(MIX), last) + 1)
                pe.wait_ge(gate_free, g * FT + (MIX + 1))
                column_tile(ps[:, 0, :], gate_tile(MIX), range(K8)).then_inc(wc_used, 1)
                gate_up(g, FT - 1, 0, last)

                def last_down(ids):
                    pe.wait_ge(wr_lo, g * NR + (NR - 1))
                    pe.wait_ge(h_lo, g * FT + (FT - 1))
                    for idx in ids:
                        pe.wait_ge(y_free, g * (CHUNKS * YN) + ((CHUNKS - 1) * YN + idx + 1))
                        y_part(CHUNKS - 1, idx, (0,))
                    pe.wait_ge(wr_lo, g * NR + NR)
                    pe.wait_ge(h_lo, g * FT + FT)
                    for idx in ids:
                        y_part(CHUNKS - 1, idx, (1,)).then_inc(y_done, 1)
                if not last:
                    def xt1(t):
                        pe.wait_ge(xn1_ready, g * NB + (NB + t + 1))
                        for h in range(2):
                            q = 2 * t + h
                            if q == 1:
                                pe.wait_ge(gate_free, g * FT + (MIX + 3))
                            elif q == 2:
                                pe.wait_ge(gate_free, g * FT + (MIX + 4))
                            elif q == 3:
                                pe.wait_ge(up_free, g * FT + (MIX + 4))
                            elif q >= 4:
                                pe.wait_ge(xt1_lo, g * 8 + (8 + q - 3))
                            xt(xn[:, t, :], h, TR_BANKS[q % 4], xt1_done)
                    xt1(0)
                    xt1(1)
                    last_down((0, 1))
                    xt1(2)
                    down(g, CHUNKS - 1, 0, (2, 3))
                    xt1(3)
                    down(g, CHUNKS - 1, 0, (4, 5, 6, 7))
                else:
                    last_down((0, 1, 2, 3))
                    down(g, CHUNKS - 1, 0, (4, 5, 6, 7))

            def xt1_first(t):
                pe.wait_ge(xn1_ready, t + 1)
                for h in range(2):
                    if t >= 2:
                        pe.wait_ge(xt1_lo, 2 * (t - 2) + h + 1)
                    xt(x1[:, t, :], h, 4 + 2 * (t % 2) + h, xt1_done)

            pe.wait_ge(consts, 1)
            pe.wait_ge(first_lo, 1 + NKV)
            kv(0, 0, range(4))
            pe.wait_ge(wc_lo, NKV)
            kv(0, 0, range(4, K8))
            kv(0, 1)
            kt(0, 0)
            xt1_first(0)
            kv(0, 2)
            kt(0, 1)
            xt1_first(1)
            xt1_first(2)
            xt1_first(3)
            kv(0, 3)
            kt(0, 2)
            kt(0, 3)
            with pe.Fori(0, NG - 1) as g:
                body(g, False)
            body(NG - 1, True)


def kernel(x, ctx_4096, g_xattn, g_ffn, L0_xattn_Wq, L0_xattn_Wk, L0_xattn_Wv, L0_xattn_Wo,
           L0_ffn_W_gate, L0_ffn_W_up, L0_ffn_W_down):
    import numpy as np
    import concourse.bacc as bacc
    from concourse.bass_utils import run_bass_kernel_spmd

    def columns(w):
        n = w.shape[1] // P
        return w.reshape(K8, P, n, P).transpose(2, 1, 0, 3).reshape(n, P, K8 * P)

    def heads(w):
        return w.reshape(D, 2, 4, GQ, HD).transpose(0, 1, 3, 2, 4).reshape(D, D)

    wq, wk, wv, wo = (np.asarray(w) for w in (L0_xattn_Wq, L0_xattn_Wk, L0_xattn_Wv, L0_xattn_Wo))
    wg, wu, wd = np.asarray(L0_ffn_W_gate).T, np.asarray(L0_ffn_W_up).T, np.asarray(L0_ffn_W_down).T
    whole = MIX * P
    order = np.r_[0:whole, F - FR:F, whole:F - FR]
    wg, wu, wd = wg[:, order], wu[:, order], wd[order]

    def gate_and_up(lo, hi):
        tiles = np.stack([columns(wg[:, lo:hi]), columns(wu[:, lo:hi])], axis=1)
        return tiles.reshape(-1, P, K8 * P)

    mix = columns(np.concatenate([wg[:, whole:whole + FR], wu[:, whole:whole + FR]], axis=1))
    wc = np.concatenate([columns(heads(wq)), columns(np.concatenate([wk, wv], axis=1)),
                         gate_and_up(0, whole), mix, gate_and_up(whole + FR, F)], axis=0)
    wo_rows = heads(wo.T).T.reshape(NO, P, D)
    short = wd[whole:whole + FR]
    wd_rows = np.concatenate([wd[:whole], short, short, wd[whole + FR:]], axis=0).reshape(FT, P, D)
    wr = np.concatenate([wo_rows, wd_rows], axis=0)
    ctx_t = np.asarray(ctx_4096).reshape(BATCH, SEQ, K8, P).transpose(0, 3, 2, 1).reshape(BATCH, P, K8 * SEQ)

    nc = bacc.Bacc("TRN2", target_bir_lowering=False, num_devices=1)
    given = {"x": np.asarray(x), "ctx_t": ctx_t, "wc": wc, "wr": wr,
             "g_xattn": np.asarray(g_xattn), "g_ffn": np.asarray(g_ffn)}
    arrays, args = {}, []
    for name, a in given.items():
        a = np.ascontiguousarray(a)
        arrays[f"in_{name}"] = a
        args.append(nc.dram_tensor(f"in_{name}", a.shape, mybir.dt.from_np(a.dtype), kind="ExternalInput").ap())
    out = nc.dram_tensor("out", (BATCH, SEQ, D), F32, kind="ExternalOutput").ap()
    gated_cross_attention_ffn(nc, *args, out)
    r = run_bass_kernel_spmd(nc, [arrays], core_ids=[0])
    return r.results[0]["out"]
```
